# Optimizing a Trainium2 kernel written in Bass

```python
import numpy as np
import jax
import jax.numpy as jnp

def _softmax(x, axis=-1):
    return jax.nn.softmax(x, axis=axis)

def _gelu(x):
    return jax.nn.gelu(x, approximate=True)

def _silu(x):
    return jax.nn.silu(x)

def _sigmoid(x):
    return jax.nn.sigmoid(x)

def _layernorm(x, axis=-1, eps=1e-05):
    m = jnp.mean(x, axis=axis, keepdims=True)
    v = jnp.var(x, axis=axis, keepdims=True)
    return (x - m) / jnp.sqrt(v + eps)

def _scatter_add(tgt, idx, src, axis=0):
    return tgt.at[idx].add(src)

def _segment_sum(src, seg, n):
    return jax.ops.segment_sum(src, seg, n)
kernel_name = 'mk_cond_resid_d2_seqx_r4_c0d4d3'

def setup_inputs(seed: int=0):
    np.random.seed(seed)
    _w = jnp.asarray

    def _rec_inputs():
        import jax
        import jax.numpy as jnp
        _rk = jax.random.key(seed)
        x = -0.0003929 + 0.9999 * jax.random.normal(jax.random.fold_in(_rk, 1), (64, 64, 256), jnp.float32)
        _lenS = 64 - jax.random.randint(jax.random.fold_in(_rk, 7), (64,), 0, max(1, 64 // 4) + 1, jnp.int32)
        _lenS2 = 64 - jax.random.randint(jax.random.fold_in(_rk, 8), (64,), 0, max(1, 64 // 4) + 1, jnp.int32)
        cond_1024 = 0.00782532 + 1.00527 * jax.random.normal(jax.random.fold_in(_rk, 11), (64, 256), jnp.float32)
        return (x, cond_1024)
    x, cond_1024 = _rec_inputs()

    def _L0_cond_setup():
        import jax, jax.numpy as jnp
        import numpy as np
        EPS = 1e-08
        key = jax.random.key(seed)
        ks = jax.random.split(key, 8)
        B, S, D, H = (8, 512, 256, 256)
        scale = 1.0 / np.sqrt(D)
        return {'input_seq': jax.random.normal(ks[0], (B, S, D), dtype=jnp.float32), 'initial_hidden': jax.random.normal(ks[1], (B, H), dtype=jnp.float32), 'W_f': jax.random.normal(ks[2], (H, D), dtype=jnp.float32) * scale, 'b_f': jnp.zeros((H,), dtype=jnp.float32), 'W_i': jax.random.normal(ks[3], (H, D), dtype=jnp.float32) * scale, 'b_i': jnp.zeros((H,), dtype=jnp.float32), 'W_h': jax.random.normal(ks[4], (H, D), dtype=jnp.float32) * scale, 'b_h': jnp.zeros((H,), dtype=jnp.float32)}
    _L0_cond_all = _L0_cond_setup()
    _L0_cond_in = {k: v for k, v in _L0_cond_all.items() if k in ('W_f', 'b_f', 'W_i', 'b_i', 'W_h', 'b_h')}
    del _L0_cond_all

    def _L1_cond_setup():
        import jax, jax.numpy as jnp
        import numpy as np
        N, T, D, H = (128, 128, 256, 256)
        key = jax.random.key(seed)
        k1, k2, k3, k4 = jax.random.split(key, 4)
        x = jax.random.normal(k1, (N, T, D), dtype=jnp.float32)
        h0 = jax.random.normal(k2, (N, H), dtype=jnp.float32)
        Wx = jax.random.normal(k3, (D, H), dtype=jnp.float32) / np.sqrt(D)
        Wh = jax.random.normal(k4, (H, H), dtype=jnp.float32) / np.sqrt(H)
        b = jnp.zeros((H,), dtype=jnp.float32)
        return {'x': x, 'h0': h0, 'Wx': Wx, 'Wh': Wh, 'b': b}
    _L1_cond_all = _L1_cond_setup()
    _L1_cond_in = {k: v for k, v in _L1_cond_all.items() if k in ('Wx', 'Wh', 'b')}
    del _L1_cond_all
    return {'x': x, 'cond_1024': cond_1024, 'L0_cond_W_f': _L0_cond_in['W_f'], 'L0_cond_b_f': _L0_cond_in['b_f'], 'L0_cond_W_i': _L0_cond_in['W_i'], 'L0_cond_b_i': _L0_cond_in['b_i'], 'L0_cond_W_h': _L0_cond_in['W_h'], 'L0_cond_b_h': _L0_cond_in['b_h'], 'L1_cond_Wx': _L1_cond_in['Wx'], 'L1_cond_Wh': _L1_cond_in['Wh'], 'L1_cond_b': _L1_cond_in['b']}

def reference(x, cond_1024, L0_cond_W_f, L0_cond_b_f, L0_cond_W_i, L0_cond_b_i, L0_cond_W_h, L0_cond_b_h, L1_cond_Wx, L1_cond_Wh, L1_cond_b):
    import jax
    import jax.numpy as jnp

    def _L0_cond_ref(input_seq, initial_hidden, W_f, b_f, W_i, b_i, W_h, b_h):
        import jax, jax.numpy as jnp
        import numpy as np
        EPS = 1e-08
        forget_gate = jax.nn.sigmoid(jnp.einsum('bsd,hd->bsh', input_seq, W_f) + b_f)
        input_gate = jax.nn.sigmoid(jnp.einsum('bsd,hd->bsh', input_seq, W_i) + b_i)
        gate_sum = forget_gate + input_gate + EPS
        forget_norm = forget_gate / gate_sum
        input_norm = input_gate / gate_sum
        candidate = jnp.einsum('bsd,hd->bsh', input_seq, W_h) + b_h
        new_info = input_norm * candidate
        log_ret = jnp.log(forget_norm + EPS)
        log_cumprod = jnp.cumsum(log_ret, axis=1)
        B, _, H = log_cumprod.shape
        padded = jnp.concatenate([jnp.zeros((B, 1, H), dtype=log_cumprod.dtype), log_cumprod], axis=1)
        scaling = jnp.exp(log_cumprod[:, -1:, :] - padded[:, :-1, :])
        hidden = jnp.cumsum(scaling * new_info, axis=1)
        hidden = hidden + jnp.exp(log_cumprod) * initial_hidden[:, None, :]
        return hidden

    def _L1_cond_ref(x, h0, Wx, Wh, b):
        import jax, jax.numpy as jnp
        import numpy as np
        N, T, D, H = (128, 128, 256, 256)
        xp = jnp.einsum('ntd,dh->nth', x, Wx) + b

        def step(prev_h, xp_t):
            next_h = jnp.tanh(xp_t + prev_h @ Wh)
            return (next_h, next_h)
        _, h = jax.lax.scan(step, h0, jnp.swapaxes(xp, 0, 1))
        return jnp.swapaxes(h, 0, 1)
    x = x + _L0_cond_ref(x, cond_1024, L0_cond_W_f, L0_cond_b_f, L0_cond_W_i, L0_cond_b_i, L0_cond_W_h, L0_cond_b_h)
    x = x + _L1_cond_ref(x, cond_1024, L1_cond_Wx, L1_cond_Wh, L1_cond_b)
    return x

_drawn_inputs = setup_inputs


def setup_inputs(seed=0):
    import zlib

    import numpy as np

    out = dict(_drawn_inputs(seed))
    spreads = {'L0_cond_b_f': (0.0, 0.8),
     'L0_cond_b_i': (0.0, 0.8),
     'L0_cond_b_h': (0.0, 0.8),
     'L1_cond_b': (0.0, 0.1)}
    factors = {}
    for name, (base, spread) in spreads.items():
        noise = np.random.default_rng([zlib.crc32(name.encode()), seed]).standard_normal(out[name].shape)
        drawn = base * np.exp(spread * noise) if base else spread * noise
        out[name] = jnp.asarray(drawn.astype(out[name].dtype))
    for name, factor in factors.items():
        out[name] = (out[name] * factor).astype(out[name].dtype)
    return out
```

```python
from contextlib import ExitStack

import concourse.bass as bass
from concourse import mybir

F32 = mybir.dt.float32
F32R = mybir.dt.float32r
BF16 = mybir.dt.bfloat16
ALU = mybir.AluOpType
ACT = mybir.ActivationFunctionType

P = 128
B = 64
S = 64
D = 256
HALVES = D // P
T = 8
NCH = S // T
COLS = T * B
CH = HALVES * COLS
RING = 4
EPS = 1e-8


def build(nc, x, cond, w_f, b_f, w_i, b_i, w_h, b_h, wx, wh, b_x, out):
    with ExitStack() as ctx:
        def sb(name, shape, dt=F32):
            return ctx.enter_context(nc.sbuf_tensor(name, shape, dt))

        def sem(name):
            return ctx.enter_context(nc.semaphore(name))

        x_rows = sb("x_rows", [P, 2, T // 2 * D])
        o_rows = x_rows
        x_hi = sb("x_hi", [P, NCH, HALVES, COLS], F32R)
        x_lo = sb("x_lo", [P, NCH, HALVES, COLS], F32R)
        r_d = sb("r_d", [P, NCH + 1, HALVES, COLS])
        q_s = sb("q_s", [P, NCH, HALVES, COLS])
        den = sb("den", [P, RING, HALVES, COLS])
        suf = sb("suf", [P, 2, HALVES, COLS])
        h_t = sb("h_t", [P, 2, HALVES, COLS])
        w_rows = h_t[:, :, :, :].rearrange("p n a c -> p (n a c)")[:, 0:3 * HALVES * D]\
            .rearrange("p (g a d) -> p g a d", g=3, a=HALVES)
        wt_hi = sb("wt_hi", [P, 3, HALVES, D], F32R)
        wt_lo = sb("wt_lo", [P, 3, HALVES, D], F32R)
        wx_f = sb("wx_f", [P, HALVES, D])
        wx_hi = sb("wx_hi", [P, HALVES, D], F32R)
        wx_lo = sb("wx_lo", [P, HALVES, D], F32R)
        wh_f = sb("wh_f", [P, HALVES, D])
        cond_rows = sb("cond_rows", [B, D])
        bias = sb("bias", [P, 3, HALVES])
        bx_rows = sb("bx_rows", [3, D])
        bx_rest = sb("bx_rest", [3, D])
        bx_part = sb("bx_part", [3, D], BF16)
        bx_part2 = sb("bx_part2", [3, D], BF16)
        bx_3 = sb("bx_3", [3, D], BF16)
        ones = sb("ones", [3, COLS], BF16)
        ident = sb("ident", [P, P])

        banks03 = ctx.enter_context(nc.psum_tensor("banks03", [P, 4, COLS], F32))
        banks47 = ctx.enter_context(nc.psum_tensor("banks47", [P, 4, COLS], F32))
        gate_ps = banks03
        xt_ps = banks47[:, :, :].rearrange("p (n a) c -> p n a c", n=2)
        xp_ps = banks03[:, :, :].rearrange("p (n a) c -> p n a c", n=2)
        cand_ps = banks47[:, 0:2, :]
        out_ps = banks47[:, 2:4, :]

        x_landed = [sem(f"x_landed{q}") for q in range(2)]
        w_landed = sem("w_landed")
        cond_landed = sem("cond_landed")
        wx_landed = sem("wx_landed")
        wh_landed = sem("wh_landed")
        bias_landed = sem("bias_landed")
        bx_landed = sem("bx_landed")
        zeroed = sem("zeroed")
        ident_ready = sem("ident_ready")
        wt_in_psum = sem("wt_in_psum")
        wt_hi_ready = sem("wt_hi_ready")
        wt_lo_ready = sem("wt_lo_ready")
        h0_ready = sem("h0_ready")
        bx_step = sem("bx_step")
        bx_ready = sem("bx_ready")
        xt_in_psum = sem("xt_in_psum")
        x_hi_ready = sem("x_hi_ready")
        x_lo_ready = sem("x_lo_ready")
        gate_in_psum = sem("gate_in_psum")
        gate_ready = sem("gate_ready")
        den_ready = sem("den_ready")
        ln_ready = sem("ln_ready")
        inv_ready = sem("inv_ready")
        u_ready = sem("u_ready")
        r_ready = sem("r_ready")
        ones_ready = sem("ones_ready")
        suf_steps = sem("suf_steps")
        i_inv_ready = sem("i_inv_ready")
        q_ready = sem("q_ready")
        cand_in_psum = sem("cand_in_psum")
        w_ready = sem("w_ready")
        s_steps = sem("s_steps")
        d_steps = sem("d_steps")
        x_sum_ready = sem("x_sum_ready")
        xd_ready = sem("xd_ready")
        x1_ready = sem("x1_ready")
        x1_hi_ready = sem("x1_hi_ready")
        x1_lo_ready = sem("x1_lo_ready")
        z_in_psum = sem("z_in_psum")
        h_ready = sem("h_ready")
        o_ready = sem("o_ready")
        o_in_psum = sem("o_in_psum")
        o_rows_ready = sem("o_rows_ready")
        o_stored = [sem(f"o_stored{q}") for q in range(2)]

        def chunk_rows(tensor, c):
            return tensor[:, c * T:(c + 1) * T, :].rearrange("b (j k) d -> j b (k d)", j=2)

        def row_tile(tile):
            return tile

        def cols(t):
            return slice(t * B, (t + 1) * B)

        def chunk_of(n):
            return NCH - 1 - n

        block = ctx.enter_context(nc.Block())

        @block.sync
        def _(sp):
            def load_x(n):
                for j in range(2):
                    sp.dma_start(x_rows[j * B:(j + 1) * B, n % 2, :], chunk_rows(x, chunk_of(n))[j])\
                        .then_inc(x_landed[n % 2], 16)

            load_x(0)
            for g, w in enumerate((w_f, w_i, w_h)):
                sp.dma_start(w_rows[:, g, :, :], w.rearrange("(a p) d -> p a d", p=P)).then_inc(w_landed, 16)
            load_x(1)
            sp.dma_start(cond_rows[:, :], cond).then_inc(cond_landed, 16)
            sp.dma_start(wx_f[:, :, :], wx.rearrange("(a p) d -> p a d", p=P)).then_inc(wx_landed, 16)
            sp.dma_start(wh_f[:, :, :], wh.rearrange("(a p) d -> p a d", p=P)).then_inc(wh_landed, 16)
            for n in range(2, NCH):
                sp.wait_ge(xt_in_psum, n - 1)
                load_x(n)
            for c in range(NCH):
                sp.wait_ge(o_rows_ready, 2 * c + 2)
                for j in range(2):
                    sp.dma_start(chunk_rows(out, c)[j], o_rows[j * B:(j + 1) * B, c % 2, :])\
                        .then_inc(o_stored[c % 2], 16)
            for q in range(2):
                sp.wait_ge(o_stored[q], 32 * (NCH // 2))

        @block.gpsimd
        def _(pool):
            nc.gpsimd.memset(ident[:, :], 0.0).then_inc(zeroed, 1)
            pool.wait_ge(zeroed, 1)
            nc.gpsimd.affine_select(out=ident[:, :], in_=ident[:, :], compare_op=ALU.not_equal, fill=1.0,
                                    base=0, pattern=[[-1, P]], channel_multiplier=1).then_inc(ident_ready, 1)

            def q_chunk(n):
                c = chunk_of(n)
                pool.wait_ge(inv_ready, n + 1)
                nc.gpsimd.tensor_tensor(q_s[:, c], q_s[:, c], den[:, n % RING], ALU.mult).then_inc(i_inv_ready, 1)
                pool.wait_ge(i_inv_ready, n + 1)
                pool.wait_ge(suf_steps, T * (n + 1))
                nc.gpsimd.tensor_tensor(q_s[:, c], q_s[:, c], suf[:, n % 2], ALU.mult).then_inc(q_ready, 1)

            for n in range(NCH):
                q_chunk(n)

            def xd_chunk(c):
                pool.wait_ge(x_lo_ready, NCH)
                if c >= RING:
                    pool.wait_ge(o_ready, 2 * (c - RING) + 2)
                pool.wait_ge(q_ready, NCH)
                nc.gpsimd.tensor_tensor(den[:, c % RING], x_hi[:, c].bitcast(F32), x_lo[:, c].bitcast(F32),
                                        ALU.add).then_inc(x_sum_ready, 1)
                for t in range(T):
                    if c or t:
                        pool.wait_ge(d_steps, T * c + t)
                    before = r_d[:, c + 1, :, cols(t - 1)] if t else r_d[:, c, :, cols(T - 1)]
                    now = r_d[:, c + 1, :, cols(t)]
                    nc.gpsimd.tensor_tensor(now, now, before, ALU.mult).then_inc(d_steps, 1)
                pool.wait_ge(x_sum_ready, c + 1)
                pool.wait_ge(d_steps, T * (c + 1))
                nc.gpsimd.tensor_tensor(den[:, c % RING], den[:, c % RING], r_d[:, c + 1], ALU.add)\
                    .then_inc(xd_ready, 1)

            pool.wait_ge(r_ready, NCH)
            pool.wait_ge(h0_ready, 2)
            for c in range(NCH):
                xd_chunk(c)

        @block.scalar
        def _(act):
            with nc.allow_non_contiguous_dma(reason="three bias vectors of 1 KB"):
                for g, b in enumerate((b_f, b_i, b_h)):
                    act.dma_start(bias[:, g, :], b.rearrange("(a p) -> p a", p=P)).then_inc(bias_landed, 16)
            for j in range(3):
                act.dma_start(bx_rows[j:j + 1, :], b_x.rearrange("(a n) -> a n", a=1)).then_inc(bx_landed, 16)

            def split_x(n):
                act.wait_ge(xt_in_psum, n + 1)
                nc.scalar.activation(x_hi[:, chunk_of(n)], xt_ps[:, n % 2], ACT.Copy).then_inc(x_hi_ready, 1)

            def sigmoids(n):
                c = chunk_of(n)
                for g in range(2):
                    for a in range(HALVES):
                        act.wait_ge(gate_in_psum, 4 * n + 2 * g + a + 1)
                        to = (r_d[:, c + 1, a], q_s[:, c, a])[g]
                        nc.scalar.activation(to, gate_ps[:, 2 * g + a], ACT.Sigmoid, bias=bias[:, g, a:a + 1])\
                            .then_inc(gate_ready, 1)

            def inverses(n):
                for k in range(n, n + 2):
                    act.wait_ge(den_ready, k + 1)
                    nc.scalar.activation(den[:, k % RING], den[:, k % RING], ACT.Ln).then_inc(ln_ready, 1)
                for k in range(n, n + 2):
                    act.wait_ge(ln_ready, k + 1)
                    nc.scalar.activation(den[:, k % RING], den[:, k % RING], ACT.Exp, scale=-1.0)\
                        .then_inc(inv_ready, 1)

            for g in range(3):
                act.wait_ge(wt_in_psum, g + 1)
                nc.scalar.activation(wt_hi[:, g], banks03[:, g].rearrange("p (a h) -> p a h", a=HALVES), ACT.Copy)\
                    .then_inc(wt_hi_ready, 1)
                if g == 0:
                    split_x(0)
            act.wait_ge(wt_in_psum, 4)
            for a in range(HALVES):
                nc.scalar.activation(r_d[:, 0, a, cols(T - 1)], banks03[:, 3, cols(a)], ACT.Copy).then_inc(h0_ready, 1)
            act.wait_ge(wx_landed, 16)
            nc.scalar.activation(wx_hi[:, :, :], wx_f[:, :, :], ACT.Copy).then_inc(wt_hi_ready, 1)
            act.wait_ge(bias_landed, 48)
            for n in range(0, NCH, 2):
                for k in range(n, n + 2):
                    if k + 1 < NCH:
                        split_x(k + 1)
                    sigmoids(k)
                inverses(n)

            def tanh(c, t):
                act.wait_ge(z_in_psum, T * c + t + 1)
                if c >= 2 and t == 0:
                    act.wait_ge(o_ready, 2 * (c - 1))
                nc.scalar.activation(h_t[:, c % 2, :, cols(t)], xp_ps[:, c % 2, :, cols(t)], ACT.Tanh)\
                    .then_inc(h_ready, 1)

            def split_x1(c, a):
                act.wait_ge(x1_ready, 2 * c + a + 1)
                nc.scalar.activation(x_hi[:, c, a], den[:, c % RING, a], ACT.Copy).then_inc(x1_hi_ready, 1)

            def out_rows(c, a):
                act.wait_ge(o_in_psum, c + 1)
                if c >= 2 and a == 0:
                    act.wait_ge(o_stored[c % 2], 32 * (c // 2))
                n = T // 4 * D
                nc.scalar.activation(o_rows[:, c % 2, a * n:(a + 1) * n], out_ps[:, a], ACT.Copy)\
                    .then_inc(o_rows_ready, 1)

            for a in range(HALVES):
                split_x1(0, a)
            for c in range(NCH):
                for t in range(T):
                    tanh(c, t)
                    if c + 1 < NCH and t in (3, 4):
                        split_x1(c + 1, t - 3)
                    if c and t in (5, 6):
                        out_rows(c - 1, t - 5)
            for a in range(HALVES):
                out_rows(NCH - 1, a)

        @block.vector
        def _(dve):
            def chunk_split(n):
                dve.wait_ge(x_hi_ready, n + 1)
                c = chunk_of(n)
                nc.vector.tensor_tensor(x_lo[:, c], xt_ps[:, n % 2], x_hi[:, c].bitcast(F32), ALU.subtract)\
                    .then_inc(x_lo_ready, 1)

            def denominator(n):
                c = chunk_of(n)
                dve.wait_ge(gate_ready, 4 * n + 4)
                if n >= RING:
                    dve.wait_ge(i_inv_ready, n - RING + 1)
                nc.vector.scalar_tensor_tensor(den[:, n % RING], r_d[:, c + 1], EPS, q_s[:, c], ALU.add, ALU.add)\
                    .then_inc(den_ready, 1)

            def ratio(n):
                c = chunk_of(n)
                dve.wait_ge(inv_ready, n + 1)
                nc.vector.tensor_tensor(r_d[:, c + 1], r_d[:, c + 1], den[:, n % RING], ALU.mult).then_inc(u_ready, 1)
                dve.wait_ge(u_ready, n + 1)
                nc.vector.tensor_scalar(r_d[:, c + 1], r_d[:, c + 1], EPS, None, ALU.add).then_inc(r_ready, 1)
                dve.wait_ge(r_ready, n + 1)

            def suffix(n, t):
                c = chunk_of(n)
                k = T - 1 - t
                if n >= 2 and k == 0:
                    dve.wait_ge(q_ready, n - 1)
                if n or k:
                    dve.wait_ge(suf_steps, T * n + k)
                after = suf[:, n % 2, :, cols(t + 1)] if t < T - 1 else suf[:, (n + 1) % 2, :, cols(0)]
                nc.vector.tensor_tensor(suf[:, n % 2, :, cols(t)], r_d[:, c + 1, :, cols(t)], after, ALU.mult)\
                    .then_inc(suf_steps, 1)

            nc.vector.memset(ones[:, :], 1.0).then_inc(ones_ready, 1)
            nc.vector.memset(suf[:, 1, :, cols(0)], 1.0).then_inc(ones_ready, 1)
            for g in range(3):
                dve.wait_ge(wt_hi_ready, g + 1)
                nc.vector.tensor_tensor(wt_lo[:, g], banks03[:, g].rearrange("p (a h) -> p a h", a=HALVES),
                                        wt_hi[:, g].bitcast(F32), ALU.subtract).then_inc(wt_lo_ready, 1)
                if g == 0:
                    chunk_split(0)
            dve.wait_ge(wt_hi_ready, 4)
            nc.vector.tensor_tensor(wx_lo[:, :, :], wx_f[:, :, :], wx_hi[:, :, :].bitcast(F32), ALU.subtract)\
                .then_inc(wt_lo_ready, 1)

            steps = [0]

            def bx(ins):
                steps[0] += 1
                ins.then_inc(bx_step, 1)
                dve.wait_ge(bx_step, steps[0])

            dve.wait_ge(bx_landed, 48)
            dve.wait_ge(ident_ready, 1)
            bx(nc.vector.tensor_copy(bx_part[:, :], bx_rows[:, :]))
            bx(nc.vector.tensor_scalar(bx_3[:, :], bx_part[:, :], ident[0:3, 0:1], None, ALU.mult))
            rest = bx_rows
            for j in (1, 2):
                bx(nc.vector.tensor_tensor(bx_rest[:, :], rest[:, :], bx_part[:, :], ALU.subtract))
                bx(nc.vector.tensor_copy(bx_part[:, :], bx_rest[:, :]))
                bx(nc.vector.tensor_scalar(bx_part2[:, :], bx_part[:, :], ident[0:3, j:j + 1], None, ALU.mult))
                bx(nc.vector.tensor_tensor(bx_3[:, :], bx_3[:, :], bx_part2[:, :], ALU.add))
                rest = bx_rest
            nc.vector.tensor_copy(bx_part[:, :], bx_3[:, :]).then_inc(bx_ready, 1)
            dve.wait_ge(ones_ready, 2)

            for n in range(0, NCH + 2, 2):
                for k in range(n, n + 2):
                    if k + 1 < NCH:
                        chunk_split(k + 1)
                    if k >= 2:
                        ratio(k - 2)
                        for t in range(T - 1, 3, -1):
                            suffix(k - 2, t)
                    if k < NCH:
                        denominator(k)
                    if k >= 2:
                        for t in range(3, -1, -1):
                            suffix(k - 2, t)

            def weighted(c, a):
                dve.wait_ge(cand_in_psum, 2 * c + a + 1)
                if a == 0:
                    dve.wait_ge(q_ready, NCH - c)
                nc.vector.scalar_tensor_tensor(q_s[:, c, a], cand_ps[:, a], bias[:, 2, a:a + 1], q_s[:, c, a],
                                               ALU.add, ALU.mult).then_inc(w_ready, 1)

            def prefix(c, t):
                if t == 0:
                    dve.wait_ge(w_ready, 2 * c + 2)
                    if c == 0:
                        return
                dve.wait_ge(s_steps, (T - 1) + T * (c - 1) + t if c else t - 1) if c or t > 1 else None
                before = q_s[:, c, :, cols(t - 1)] if t else q_s[:, c - 1, :, cols(T - 1)]
                now = q_s[:, c, :, cols(t)]
                nc.vector.tensor_tensor(now, now, before, ALU.add).then_inc(s_steps, 1)

            def first_layer(c, a):
                if a == 0:
                    dve.wait_ge(s_steps, T * (c + 1) - 1)
                    dve.wait_ge(xd_ready, c + 1)
                nc.vector.tensor_tensor(den[:, c % RING, a], den[:, c % RING, a], q_s[:, c, a], ALU.add)\
                    .then_inc(x1_ready, 1)

            def x1_rest(c, a):
                dve.wait_ge(x1_hi_ready, 2 * c + a + 1)
                nc.vector.tensor_tensor(x_lo[:, c, a], den[:, c % RING, a], x_hi[:, c, a].bitcast(F32), ALU.subtract)\
                    .then_inc(x1_lo_ready, 1)

            def out_sum(c, a):
                dve.wait_ge(h_ready, T * (c + 1))
                if c >= 2:
                    dve.wait_ge(o_in_psum, c - 1)
                to = suf[:, c % 2, a].rearrange("p (k j b) -> p j k b", j=2, k=T // 2)
                nc.vector.tensor_tensor(to, den[:, c % RING, a].rearrange("p (j k b) -> p j k b", j=2, k=T // 2),
                                        h_t[:, c % 2, a].rearrange("p (j k b) -> p j k b", j=2, k=T // 2), ALU.add)\
                    .then_inc(o_ready, 1)

            for c in range(2):
                for a in range(HALVES):
                    weighted(c, a)
            for t in range(T):
                prefix(0, t)
            for a in range(HALVES):
                first_layer(0, a)
            for a in range(HALVES):
                x1_rest(0, a)
            for c in range(NCH):
                for t in range(T):
                    if c + 1 < NCH:
                        prefix(c + 1, t)
                    if c and t in (1, 3):
                        out_sum(c - 1, t // 2)
                if c + 1 < NCH:
                    for a in range(HALVES):
                        first_layer(c + 1, a)
                if c + 2 < NCH:
                    weighted(c + 2, 0)
                if c + 1 < NCH:
                    for a in range(HALVES):
                        x1_rest(c + 1, a)
                if c + 2 < NCH:
                    weighted(c + 2, 1)
            for a in range(HALVES):
                out_sum(NCH - 1, a)

        @block.tensor
        def _(pe):
            pe.wait_ge(ident_ready, 1)
            pe.wait_ge(w_landed, 48)

            def transpose_w(g):
                for dk in range(HALVES):
                    for a in range(HALVES):
                        last = nc.tensor.transpose(banks03[:, g, dk * D + a * P:dk * D + (a + 1) * P],
                                                   w_rows[:, g, a, dk * P:(dk + 1) * P], ident[:, :])
                last.then_inc(wt_in_psum, 1)

            def transpose_x(n):
                pe.wait_ge(x_landed[n % 2], 32 * (n // 2 + 1))
                if n >= 2:
                    pe.wait_ge(x_lo_ready, n - 1)
                for k in range(T // 2):
                    for dk in range(HALVES):
                        to = xt_ps[:, n % 2, dk].rearrange("p (j k b) -> p k j b", j=2, k=T // 2)[:, k]
                        last = nc.tensor.transpose(to, x_rows[:, n % 2, k * D + dk * P:k * D + (dk + 1) * P],
                                                   ident[:, :])
                last.then_inc(xt_in_psum, 1)

            def three_passes(to, w_hi, w_lo, c, a, start, stop):
                n = 0
                for dk in range(HALVES):
                    rows = slice(a * P, (a + 1) * P)
                    for w, v in ((w_lo, x_hi), (w_hi, x_lo), (w_hi, x_hi)):
                        last = nc.tensor.matmul(to, w[:, dk, rows], v[:, c, dk], start=start and n == 0,
                                                stop=stop and n == 5, skip_group_check=True)
                        n += 1
                return last

            def gates(n):
                pe.wait_ge(x_hi_ready, n + 1)
                pe.wait_ge(x_lo_ready, n + 1)
                for g in range(2):
                    for a in range(HALVES):
                        if n:
                            pe.wait_ge(gate_ready, 4 * (n - 1) + 2 * g + a + 1)
                        three_passes(gate_ps[:, 2 * g + a], wt_hi[:, g], wt_lo[:, g], chunk_of(n), a, True, True)\
                            .then_inc(gate_in_psum, 1)

            transpose_w(0)
            transpose_x(0)
            transpose_w(1)
            transpose_w(2)
            pe.wait_ge(cond_landed, 16)
            for a in range(HALVES):
                last = nc.tensor.transpose(banks03[:, 3, cols(a)], cond_rows[:, a * P:(a + 1) * P], ident[0:B, 0:B])
            last.then_inc(wt_in_psum, 1)
            pe.wait_ge(wt_lo_ready, 3)
            pe.wait_ge(h0_ready, 2)
            for n in range(NCH):
                if n + 1 < NCH:
                    transpose_x(n + 1)
                gates(n)

            def candidate(c, a):
                if c:
                    pe.wait_ge(w_ready, 2 * (c - 1) + a + 1)
                three_passes(cand_ps[:, a], wt_hi[:, 2], wt_lo[:, 2], c, a, True, True).then_inc(cand_in_psum, 1)

            def project(c, a):
                if a == 0:
                    pe.wait_ge(x1_lo_ready, 2 * c + 2)
                nc.tensor.matmul(xp_ps[:, c % 2, a], bx_part[:, a * P:(a + 1) * P], ones[:, :], start=True, stop=False,
                                 skip_group_check=True)
                three_passes(xp_ps[:, c % 2, a], wx_hi, wx_lo, c, a, False, False)

            def step(c, t):
                if c or t:
                    pe.wait_ge(h_ready, T * c + t)
                for dk in range(HALVES):
                    if c or t:
                        before = h_t[:, (c - (t == 0)) % 2, dk, cols((t - 1) % T)]
                    else:
                        before = r_d[:, 0, dk, cols(T - 1)]
                    for a in range(HALVES):
                        last = nc.tensor.matmul(xp_ps[:, c % 2, a, cols(t)], wh_f[:, dk, a * P:(a + 1) * P], before,
                                                start=False, stop=dk == 1, skip_group_check=True)
                last.then_inc(z_in_psum, 1)

            def transpose_out(c, k):
                if k == 0:
                    pe.wait_ge(o_ready, 2 * c + 2)
                    if c:
                        pe.wait_ge(o_rows_ready, 2 * c)
                for a in range(HALVES):
                    last = nc.tensor.transpose(out_ps[:, k // 2, (k % 2) * D + a * P:(k % 2) * D + (a + 1) * P],
                                               suf[:, c % 2, a, k * P:(k + 1) * P], ident[:, :])
                if k == T // 2 - 1:
                    last.then_inc(o_in_psum, 1)

            pe.wait_ge(x_hi_ready, NCH)
            pe.wait_ge(x_lo_ready, NCH)
            for c in range(2):
                for a in range(HALVES):
                    candidate(c, a)
            pe.wait_ge(gate_ready, 4 * NCH)
            pe.wait_ge(wt_lo_ready, 4)
            pe.wait_ge(bx_ready, 1)
            pe.wait_ge(wh_landed, 16)
            for a in range(HALVES):
                project(0, a)
            for c in range(NCH):
                for t in range(T):
                    step(c, t)
                    if c + 2 < NCH and t in (0, 2):
                        candidate(c + 2, t // 2)
                    if c and t in (2, 3, 4, 5):
                        transpose_out(c - 1, t - 2)
                    if c + 1 < NCH and t in (5, 6):
                        project(c + 1, t - 5)
            for k in range(T // 2):
                transpose_out(NCH - 1, k)


_INS = ['x', 'cond_1024', 'L0_cond_W_f', 'L0_cond_b_f', 'L0_cond_W_i', 'L0_cond_b_i', 'L0_cond_W_h', 'L0_cond_b_h',
        'L1_cond_Wx', 'L1_cond_Wh', 'L1_cond_b']


def kernel(**inputs):
    import numpy as np
    import concourse.bacc as bacc
    from concourse.bass_utils import run_bass_kernel_spmd

    nc = bacc.Bacc("TRN2", target_bir_lowering=False, num_devices=1)
    arrays, args = {}, []
    for name in _INS:
        a = np.ascontiguousarray(inputs[name])
        arrays[f"in_{name}"] = a
        args.append(nc.dram_tensor(f"in_{name}", a.shape, mybir.dt.from_np(a.dtype), kind="ExternalInput").ap())
    out = nc.dram_tensor("out_x", (B, S, D), F32, kind="ExternalOutput").ap()
    build(nc, *args, out)
    result = run_bass_kernel_spmd(nc, [arrays], core_ids=[0])
    return result.results[0]["out_x"]
```

```python
from contextlib import ExitStack

import concourse.bass as bass
from concourse import mybir

F32 = mybir.dt.float32
F32R = mybir.dt.float32r
BF16 = mybir.dt.bfloat16
ALU = mybir.AluOpType
ACT = mybir.ActivationFunctionType

P = 128
B = 64
S = 64
D = 256
HALVES = D // P
T = 8
NCH = S // T
COLS = T * B
CH = HALVES * COLS
RING = 4
SUF = 3
EPS = 1e-8


def build(nc, x, cond, w_f, b_f, w_i, b_i, w_h, b_h, wx, wh, b_x, out):
    with ExitStack() as ctx:
        def sb(name, shape, dt=F32):
            return ctx.enter_context(nc.sbuf_tensor(name, shape, dt))

        def sem(name):
            return ctx.enter_context(nc.semaphore(name))

        x_rows = sb("x_rows", [P, 2, T // 2 * D])
        o_rows = x_rows
        d_first = x_rows[:, 0, :].rearrange("p (a c) -> p a c", a=2)
        x_hi = sb("x_hi", [P, NCH, HALVES, COLS], F32R)
        x_lo = sb("x_lo", [P, NCH, HALVES, COLS], F32R)
        r_d = sb("r_d", [P, NCH + 1, HALVES, COLS])
        q_s = sb("q_s", [P, NCH, HALVES, COLS])
        den = sb("den", [P, RING, HALVES, COLS])
        suf = sb("suf", [P, SUF, HALVES, COLS])
        h_t = sb("h_t", [P, 2, HALVES, COLS])
        w_rows = h_t[:, :, :, :].rearrange("p n a c -> p (n a c)")[:, 0:3 * HALVES * D]\
            .rearrange("p (g a d) -> p g a d", g=3, a=HALVES)
        wt_hi = sb("wt_hi", [P, 3, HALVES, D], F32R)
        wt_lo = sb("wt_lo", [P, 3, HALVES, D], F32R)
        wx_f = sb("wx_f", [P, HALVES, D])
        wx_hi = sb("wx_hi", [P, HALVES, D], F32R)
        wx_lo = sb("wx_lo", [P, HALVES, D], F32R)
        wh_f = sb("wh_f", [P, HALVES, D])
        cond_rows = sb("cond_rows", [B, D])
        bias = sb("bias", [P, 3, HALVES])
        bx_rows = sb("bx_rows", [3, D])
        bx_rest = sb("bx_rest", [3, D])
        bx_part = sb("bx_part", [3, D], BF16)
        bx_part2 = sb("bx_part2", [3, D], BF16)
        bx_3 = sb("bx_3", [3, D], BF16)
        ones = sb("ones", [3, COLS], BF16)
        ident = sb("ident", [P, P])
        eps_col = sb("eps_col", [P, 1])
        first = sb("first", [P, 1])

        ps = ctx.enter_context(nc.psum_tensor("ps", [P, 8, COLS], F32))
        XT, CAND = 4, 6

        x_landed = [sem(f"x_landed{q}") for q in range(2)]
        w_landed = [sem(f"w_landed{g}") for g in range(3)]
        cond_landed = sem("cond_landed")
        wx_landed = sem("wx_landed")
        wh_landed = sem("wh_landed")
        bias_landed = sem("bias_landed")
        bx_landed = sem("bx_landed")
        zeroed = sem("zeroed")
        ident_ready = sem("ident_ready")
        wt_in_psum = sem("wt_in_psum")
        wt_hi_ready = sem("wt_hi_ready")
        wt_lo_ready = sem("wt_lo_ready")
        h0_ready = sem("h0_ready")
        bx_step = sem("bx_step")
        bx_ready = sem("bx_ready")
        xt_in_psum = sem("xt_in_psum")
        x_hi_ready = sem("x_hi_ready")
        x_lo_ready = sem("x_lo_ready")
        gate_in_psum = sem("gate_in_psum")
        gate_ready = sem("gate_ready")
        den_ready = sem("den_ready")
        ln_ready = sem("ln_ready")
        inv_ready = sem("inv_ready")
        u_ready = sem("u_ready")
        r_ready = sem("r_ready")
        r_last_ready = sem("r_last_ready")
        ones_ready = sem("ones_ready")
        suf_steps = sem("suf_steps")
        i_inv_ready = sem("i_inv_ready")
        q_ready = sem("q_ready")
        q_last_ready = sem("q_last_ready")
        cand_in_psum = sem("cand_in_psum")
        w_ready = [sem(f"w_ready{a}") for a in range(HALVES)]
        w_first_ready = sem("w_first_ready")
        w_second_ready = sem("w_second_ready")
        cand_moved = sem("cand_moved")
        w_moved_ready = sem("w_moved_ready")
        s_steps = sem("s_steps")
        d_steps = sem("d_steps")
        x_sum_ready = sem("x_sum_ready")
        xd_ready = sem("xd_ready")
        x1_ready = sem("x1_ready")
        x1_hi_ready = sem("x1_hi_ready")
        x1_lo_ready = sem("x1_lo_ready")
        z_in_psum = sem("z_in_psum")
        h_ready = sem("h_ready")
        o_ready = sem("o_ready")
        o_in_psum = sem("o_in_psum")
        o_rows_ready = sem("o_rows_ready")
        o_stored = [sem(f"o_stored{q}") for q in range(2)]

        def chunk_rows(tensor, c):
            return tensor[:, c * T:(c + 1) * T, :].rearrange("b (j k) d -> j b (k d)", j=2)

        def cols(t, n=1):
            return slice(t * B, (t + n) * B)

        def half_cols(th):
            return cols(th * T // 2, T // 2)

        def d_of(c):
            return d_first if c == 0 else r_d[:, c + 1]

        def chunk_of(n):
            return NCH - 1 - n

        CAND_ORDER = [7, 6, 5, 0, 4, 3, 1, 2]
        CAND_BANK = [CAND, CAND, CAND, XT, 0, 2, CAND, 0]
        EARLY_AFTER = {2: 0, 4: 1, 6: 2}
        EARLY = len(EARLY_AFTER)
        SPLIT_STEPS = [(4, 5), (3, 4), (0, 1)]
        OUT_STEPS = [(), (4, 5), (2, 3)]
        MOVED = {4: x_rows[:, 1, :].rearrange("p (a c) -> p a c", a=2), 3: h_t[:, 1], 2: den[:, RING - 1]}
        MOVED_ORDER = list(MOVED)

        block = ctx.enter_context(nc.Block())

        @block.sync
        def _(sp):
            def load_x(n):
                for j in range(2):
                    sp.dma_start(x_rows[j * B:(j + 1) * B, n % 2, :], chunk_rows(x, chunk_of(n))[j])\
                        .then_inc(x_landed[n % 2], 16)

            load_x(0)
            for g, w in enumerate((w_f, w_i)):
                sp.dma_start(w_rows[:, g, :, :], w.rearrange("(a p) d -> p a d", p=P)).then_inc(w_landed[g], 16)
            load_x(1)
            sp.dma_start(w_rows[:, 2, :, :], w_h.rearrange("(a p) d -> p a d", p=P)).then_inc(w_landed[2], 16)
            sp.dma_start(cond_rows[:, :], cond).then_inc(cond_landed, 16)
            sp.dma_start(wx_f[:, :, :], wx.rearrange("(a p) d -> p a d", p=P)).then_inc(wx_landed, 16)
            sp.dma_start(wh_f[:, :, :], wh.rearrange("(a p) d -> p a d", p=P)).then_inc(wh_landed, 16)
            for n in range(2, NCH):
                sp.wait_ge(xt_in_psum, n - 1)
                load_x(n)
            for c in range(NCH):
                sp.wait_ge(o_rows_ready, 2 * c + 2)
                for j in range(2):
                    sp.dma_start(chunk_rows(out, c)[j], o_rows[j * B:(j + 1) * B, c % 2, :])\
                        .then_inc(o_stored[c % 2], 16)
            for q in range(2):
                sp.wait_ge(o_stored[q], 32 * (NCH // 2))

        @block.gpsimd
        def _(pool):
            nc.gpsimd.memset(ident[:, :], 0.0).then_inc(zeroed, 1)
            pool.wait_ge(zeroed, 1)
            nc.gpsimd.affine_select(out=ident[:, :], in_=ident[:, :], compare_op=ALU.not_equal, fill=1.0,
                                    base=0, pattern=[[-1, P]], channel_multiplier=1).then_inc(ident_ready, 1)

            def i_by_den(n):
                pool.wait_ge(inv_ready, n + 1)
                nc.gpsimd.tensor_tensor(q_s[:, chunk_of(n)], q_s[:, chunk_of(n)], den[:, n % RING], ALU.mult)\
                    .then_inc(i_inv_ready, 1)

            def q_chunk(n):
                pool.wait_ge(i_inv_ready, n + 1)
                pool.wait_ge(suf_steps, T * (n + 1))
                nc.gpsimd.tensor_tensor(q_s[:, chunk_of(n)], q_s[:, chunk_of(n)], suf[:, n % SUF], ALU.mult)\
                    .then_inc(q_ready, 1)

            def x_sum(c):
                pool.wait_ge(x_lo_ready, NCH)
                if c >= RING:
                    pool.wait_ge(o_ready, 2 * (c - RING) + 2)
                else:
                    pool.wait_ge(i_inv_ready, NCH - RING + c + 1 if c < RING // 2 else NCH)
                    pool.wait_ge(u_ready, NCH - RING + c + 1)
                if c == RING - 1:
                    pool.wait_ge(w_moved_ready, MOVED_ORDER.index(2) + 1)
                nc.gpsimd.tensor_tensor(den[:, c % RING], x_hi[:, c].bitcast(F32), x_lo[:, c].bitcast(F32),
                                        ALU.add).then_inc(x_sum_ready, 1)

            def d_half(c, th):
                for t in range(th * T // 2, (th + 1) * T // 2):
                    if c or t:
                        pool.wait_ge(d_steps, T * c + t)
                    before = d_of(c)[:, :, cols(t - 1)] if t else d_of(c - 1)[:, :, cols(T - 1)]
                    nc.gpsimd.tensor_tensor(d_of(c)[:, :, cols(t)], d_of(c)[:, :, cols(t)], before, ALU.mult)\
                        .then_inc(d_steps, 1)
                pool.wait_ge(x_sum_ready, c + 1)
                pool.wait_ge(d_steps, T * c + (th + 1) * T // 2)
                nc.gpsimd.tensor_tensor(den[:, c % RING, :, half_cols(th)], den[:, c % RING, :, half_cols(th)],
                                        d_of(c)[:, :, half_cols(th)], ALU.add).then_inc(xd_ready, 1)

            def plus_eps(n):
                c = chunk_of(n)
                pool.wait_ge(suf_steps, T * (n + 1))
                nc.gpsimd.tensor_scalar(r_d[:, c + 1], r_d[:, c + 1], 1.0, EPS, ALU.mult, ALU.add).then_inc(r_ready, 1)

            i_by_den(0)
            for n in range(NCH - 3):
                i_by_den(n + 1)
                q_chunk(n)
                plus_eps(n)
            x_sum(0)
            x_sum(1)
            i_by_den(NCH - 1)
            pool.wait_ge(r_last_ready, 1)
            pool.wait_ge(h0_ready, 2)
            d_half(0, 0)
            i_by_den(NCH - 2)
            d_half(0, 1)
            pool.wait_ge(r_last_ready, 3)
            d_half(1, 0)
            d_half(1, 1)
            q_chunk(NCH - 3)
            pool.wait_ge(r_ready, NCH - 3)
            for c in range(2, NCH):
                x_sum(c)
                d_half(c, 0)
                d_half(c, 1)

        @block.scalar
        def _(act):
            act.wait_ge(ones_ready, 1)
            nc.scalar.activation(first[:, :], first[:, :], ACT.Sigmoid)
            with nc.allow_non_contiguous_dma(reason="three bias vectors of 1 KB"):
                for g, b in enumerate((b_f, b_i, b_h)):
                    act.dma_start(bias[:, g, :], b.rearrange("(a p) -> p a", p=P)).then_inc(bias_landed, 16)
            for j in range(3):
                act.dma_start(bx_rows[j:j + 1, :], b_x.rearrange("(a n) -> a n", a=1)).then_inc(bx_landed, 16)

            def split_x(n):
                act.wait_ge(xt_in_psum, n + 1)
                nc.scalar.activation(x_hi[:, chunk_of(n)], ps[:, XT:XT + 2], ACT.Copy).then_inc(x_hi_ready, 1)

            def split_w(g):
                act.wait_ge(wt_in_psum, g + 1)
                nc.scalar.activation(wt_hi[:, g], ps[:, g].rearrange("p (a h) -> p a h", a=HALVES), ACT.Copy)\
                    .then_inc(wt_hi_ready, 1)

            def sigmoids(n):
                c = chunk_of(n)
                for g in range(2):
                    for a in range(HALVES):
                        act.wait_ge(gate_in_psum, 4 * n + 2 * g + a + 1)
                        to = (r_d[:, c + 1, a], q_s[:, c, a])[g]
                        nc.scalar.activation(to, ps[:, 2 * g + a], ACT.Sigmoid, bias=bias[:, g, a:a + 1])\
                            .then_inc(gate_ready, 1)

            def inverses(n):
                nc.scalar.preload_act_table_set("natural_log_exp_and_others")
                for k in range(n, n + 2):
                    act.wait_ge(den_ready, k + 1)
                    nc.scalar.activation(den[:, k % RING], den[:, k % RING], ACT.Ln).then_inc(ln_ready, 1)
                    if k == n and n + 3 < NCH:
                        split_x(n + 3)
                for k in range(n, n + 2):
                    act.wait_ge(ln_ready, k + 1)
                    nc.scalar.activation(den[:, k % RING], den[:, k % RING], ACT.Exp, scale=-1.0)\
                        .then_inc(inv_ready, 1)

            split_w(0)
            split_x(0)
            split_w(1)
            split_w(2)
            act.wait_ge(wt_in_psum, 4)
            for a in range(HALVES):
                nc.scalar.activation(r_d[:, 0, a, cols(T - 1)], ps[:, 3, cols(a)], ACT.Copy).then_inc(h0_ready, 1)
            act.wait_ge(wx_landed, 16)
            nc.scalar.activation(wx_hi[:, :, :], wx_f[:, :, :], ACT.Copy).then_inc(wt_hi_ready, 1)
            act.wait_ge(bias_landed, 48)
            split_x(1)
            for n in range(0, NCH, 2):
                sigmoids(n)
                if n + 2 < NCH:
                    split_x(n + 2)
                sigmoids(n + 1)
                inverses(n)

            def tanh(c, t):
                if c >= 2 and t == 0:
                    act.wait_ge(o_ready, 2 * (c - 1))
                if c == 1 and t == 0:
                    act.wait_ge(w_moved_ready, MOVED_ORDER.index(3) + 1)
                for a in range(HALVES):
                    act.wait_ge(z_in_psum, HALVES * (T * c + t) + a + 1)
                    nc.scalar.activation(h_t[:, c % 2, a, cols(t)],
                                         ps[:, 4 * (c % 2) + 2 * a + t % 2, cols(t // 2)], ACT.Tanh)\
                        .then_inc(h_ready, 1)

            def split_x1(c, th):
                act.wait_ge(x1_ready, 2 * c + th + 1)
                nc.scalar.activation(x_hi[:, c, :, half_cols(th)], den[:, c % RING, :, half_cols(th)], ACT.Copy)\
                    .then_inc(x1_hi_ready, 1)

            def out_rows(c, part):
                act.wait_ge(o_in_psum, T // 2 * c + 2 * part + 2)
                if c == 1 and part == 0:
                    act.wait_ge(w_moved_ready, MOVED_ORDER.index(4) + 1)
                if c >= 2 and part == 0:
                    act.wait_ge(o_stored[c % 2], 32 * (c // 2))
                banks = slice(4 * (c % 2) + 2 * part, 4 * (c % 2) + 2 * part + 2)
                to = o_rows[:, c % 2, 2 * part * D:2 * (part + 1) * D].rearrange("p (k d) -> p k d", k=2)
                nc.scalar.activation(to, ps[:, banks, D:2 * D], ACT.Copy).then_inc(o_rows_ready, 1)

            def move_candidate(c):
                for a in range(HALVES):
                    m = CAND_ORDER.index(c)
                    act.wait_ge(cand_in_psum, 2 * m + a + 1)
                    nc.scalar.activation(MOVED[c][:, a], ps[:, CAND_BANK[m] + a], ACT.Identity,
                                         bias=bias[:, 2, a:a + 1]).then_inc(cand_moved, 1)

            nc.scalar.preload_act_table_set("sigmoid_and_others")
            act.wait_ge(xt_in_psum, NCH)
            def plus_eps(c):
                if c:
                    act.wait_ge(suf_steps, T * (NCH - c))
                else:
                    act.wait_ge(u_ready, NCH)
                nc.scalar.activation(d_of(c), r_d[:, c + 1], ACT.Identity, bias=eps_col[:, 0:1])\
                    .then_inc(r_last_ready, 1)

            move_candidate(4)
            move_candidate(3)
            plus_eps(0)
            plus_eps(2)
            plus_eps(1)
            act.wait_ge(i_inv_ready, NCH - 1)
            act.wait_ge(u_ready, NCH)
            move_candidate(2)
            split_x1(0, 0)
            split_x1(0, 1)
            for c in range(NCH):
                for t in range(T):
                    tanh(c, t)
                    if c + 1 < NCH and t in SPLIT_STEPS[min(c, 2)]:
                        split_x1(c + 1, SPLIT_STEPS[min(c, 2)].index(t))
                    if c and t in OUT_STEPS[min(c, 2)]:
                        out_rows(c - 1, OUT_STEPS[min(c, 2)].index(t))
            out_rows(NCH - 1, 0)
            out_rows(NCH - 1, 1)

        @block.vector
        def _(dve):
            def chunk_split(n):
                dve.wait_ge(x_hi_ready, n + 1)
                c = chunk_of(n)
                nc.vector.tensor_tensor(x_lo[:, c], ps[:, XT:XT + 2], x_hi[:, c].bitcast(F32), ALU.subtract)\
                    .then_inc(x_lo_ready, 1)

            def weight_split(g):
                dve.wait_ge(wt_hi_ready, g + 1)
                nc.vector.tensor_tensor(wt_lo[:, g], ps[:, g].rearrange("p (a h) -> p a h", a=HALVES),
                                        wt_hi[:, g].bitcast(F32), ALU.subtract).then_inc(wt_lo_ready, 1)

            def denominator(n):
                c = chunk_of(n)
                dve.wait_ge(gate_ready, 4 * n + 4)
                if n >= RING:
                    dve.wait_ge(i_inv_ready, n - RING + 1)
                nc.vector.scalar_tensor_tensor(den[:, n % RING], r_d[:, c + 1], EPS, q_s[:, c], ALU.add, ALU.add)\
                    .then_inc(den_ready, 1)

            def ratio(n):
                c = chunk_of(n)
                dve.wait_ge(inv_ready, n + 1)
                nc.vector.tensor_tensor(r_d[:, c + 1], r_d[:, c + 1], den[:, n % RING], ALU.mult).then_inc(u_ready, 1)
                dve.wait_ge(u_ready, n + 1)

            def suffix(n, t):
                c = chunk_of(n)
                k = T - 1 - t
                if n >= SUF and k == 0:
                    dve.wait_ge(q_ready, n - SUF + 1)
                if n or k:
                    dve.wait_ge(suf_steps, T * n + k)
                after = suf[:, n % SUF, :, cols(t + 1)] if t < T - 1 else suf[:, (n - 1) % SUF, :, cols(0)]
                nc.vector.scalar_tensor_tensor(suf[:, n % SUF, :, cols(t)], r_d[:, c + 1, :, cols(t)], EPS, after,
                                               ALU.add, ALU.mult).then_inc(suf_steps, 1)

            def weighted(m, a):
                dve.wait_ge(cand_in_psum, 2 * m + a + 1)
                c = CAND_ORDER[m]
                if c >= 2:
                    dve.wait_ge(q_ready, NCH - c)
                else:
                    dve.wait_ge(q_last_ready, 3)
                ready = w_ready[a] if c >= 2 else w_second_ready
                nc.vector.scalar_tensor_tensor(q_s[:, c, a], ps[:, CAND_BANK[m] + a], bias[:, 2, a:a + 1], q_s[:, c, a],
                                               ALU.add, ALU.mult).then_inc(ready, 1)

            def weighted_first(th):
                dve.wait_ge(q_last_ready, 1 + th)
                for a in range(HALVES):
                    dve.wait_ge(cand_in_psum, 2 * CAND_ORDER.index(0) + a + 1)
                    nc.vector.scalar_tensor_tensor(q_s[:, 0, a, half_cols(th)],
                                                   ps[:, CAND_BANK[CAND_ORDER.index(0)] + a, half_cols(th)],
                                                   bias[:, 2, a:a + 1], q_s[:, 0, a, half_cols(th)],
                                                   ALU.add, ALU.mult).then_inc(w_first_ready, 1)

            def q_last(c, th=None):
                at = half_cols(th) if th is not None else slice(0, COLS)
                dve.wait_ge(i_inv_ready, NCH - 1 + c)
                dve.wait_ge(suf_steps, T * NCH)
                nc.vector.tensor_tensor(q_s[:, c, :, at], q_s[:, c, :, at], suf[:, chunk_of(c) % SUF, :, at], ALU.mult)\
                    .then_inc(q_last_ready, 1)

            def prefix(c, t):
                if c == 0 and t == 0:
                    return
                if c or t > 1:
                    dve.wait_ge(s_steps, T * c + t - 1)
                before = q_s[:, c, :, cols(t - 1)] if t else q_s[:, c - 1, :, cols(T - 1)]
                now = q_s[:, c, :, cols(t)]
                nc.vector.tensor_tensor(now, now, before, ALU.add).then_inc(s_steps, 1)

            def first_layer(c, th):
                dve.wait_ge(s_steps, T * c + (th + 1) * T // 2 - 1)
                dve.wait_ge(xd_ready, 2 * c + th + 1)
                nc.vector.tensor_tensor(den[:, c % RING, :, half_cols(th)], den[:, c % RING, :, half_cols(th)],
                                        q_s[:, c, :, half_cols(th)], ALU.add).then_inc(x1_ready, 1)

            def x1_rest(c, th):
                dve.wait_ge(x1_hi_ready, 2 * c + th + 1)
                nc.vector.tensor_tensor(x_lo[:, c, :, half_cols(th)], den[:, c % RING, :, half_cols(th)],
                                        x_hi[:, c, :, half_cols(th)].bitcast(F32), ALU.subtract)\
                    .then_inc(x1_lo_ready, 1)

            def out_sum(c, th):
                dve.wait_ge(h_ready, HALVES * (T * c + (th + 1) * T // 2))
                if c >= 2 and th == 0:
                    dve.wait_ge(o_in_psum, T // 2 * (c - 1))
                to = suf[:, c % 2].rearrange("p a (k j b) -> p j a k b", j=2, k=T // 2)[:, th]
                x1 = den[:, c % RING, :, half_cols(th)].rearrange("p a (k b) -> p a k b", b=B)
                h = h_t[:, c % 2, :, half_cols(th)].rearrange("p a (k b) -> p a k b", b=B)
                nc.vector.tensor_tensor(to, x1, h, ALU.add).then_inc(o_ready, 1)

            nc.vector.memset(first[:, :], 0.0).then_inc(ones_ready, 1)
            nc.vector.memset(eps_col[:, :], EPS).then_inc(ones_ready, 1)
            nc.vector.memset(ones[:, :], 1.0).then_inc(ones_ready, 1)
            nc.vector.memset(suf[:, SUF - 1, :, cols(0)], 1.0).then_inc(ones_ready, 1)
            weight_split(0)
            chunk_split(0)
            weight_split(1)
            weight_split(2)
            dve.wait_ge(wt_hi_ready, 4)
            nc.vector.tensor_tensor(wx_lo[:, :, :], wx_f[:, :, :], wx_hi[:, :, :].bitcast(F32), ALU.subtract)\
                .then_inc(wt_lo_ready, 1)

            steps = [0]

            def bx(ins):
                steps[0] += 1
                ins.then_inc(bx_step, 1)
                dve.wait_ge(bx_step, steps[0])

            dve.wait_ge(bx_landed, 48)
            dve.wait_ge(ident_ready, 1)
            bx(nc.vector.tensor_copy(bx_part[:, :], bx_rows[:, :]))
            bx(nc.vector.tensor_scalar(bx_3[:, :], bx_part[:, :], ident[0:3, 0:1], None, ALU.mult))
            rest = bx_rows
            for j in (1, 2):
                bx(nc.vector.tensor_tensor(bx_rest[:, :], rest[:, :], bx_part[:, :], ALU.subtract))
                bx(nc.vector.tensor_copy(bx_part[:, :], bx_rest[:, :]))
                bx(nc.vector.tensor_scalar(bx_part2[:, :], bx_part[:, :], ident[0:3, j:j + 1], None, ALU.mult))
                bx(nc.vector.tensor_tensor(bx_3[:, :], bx_3[:, :], bx_part2[:, :], ALU.add))
                rest = bx_rest
            nc.vector.tensor_copy(bx_part[:, :], bx_3[:, :]).then_inc(bx_ready, 1)
            dve.wait_ge(ones_ready, 4)

            def product(m):
                for a in range(HALVES):
                    weighted(m, a)

            def suffixes(n):
                for t in range(T - 1, -1, -1):
                    suffix(n, t)

            chunk_split(1)
            for n in range(0, NCH, 2):
                if n:
                    ratio(n - 2)
                denominator(n)
                if n + 2 < NCH:
                    chunk_split(n + 2)
                if n:
                    suffixes(n - 2)
                if n >= 4:
                    product(n // 2 - 1)
                denominator(n + 1)
                if n + 3 < NCH:
                    chunk_split(n + 3)
                if n == 2:
                    product(0)
                if n:
                    ratio(n - 1)
                    suffixes(n - 1)
            ratio(NCH - 2)
            ratio(NCH - 1)
            suffixes(NCH - 2)
            suffixes(NCH - 1)
            for th in range(2):
                q_last(0, th)
                weighted_first(th)
                for t in range(th * T // 2, (th + 1) * T // 2):
                    if t == 1 or t == T // 2:
                        dve.wait_ge(w_first_ready, 2 * th + 2)
                    prefix(0, t)
                first_layer(0, th)
                x1_rest(0, th)
            q_last(1)
            product(CAND_ORDER.index(1))
            dve.wait_ge(w_second_ready, 2)
            for t in range(T):
                prefix(1, t)
            for th in range(2):
                first_layer(1, th)
            for th in range(2):
                x1_rest(1, th)
            for n, c in enumerate(MOVED_ORDER):
                dve.wait_ge(cand_moved, 2 * n + 2)
                dve.wait_ge(q_ready, NCH - c)
                nc.vector.tensor_tensor(q_s[:, c], q_s[:, c], MOVED[c], ALU.mult).then_inc(w_moved_ready, 1)
            dve.wait_ge(w_moved_ready, 3)
            for c in range(NCH):
                if c:
                    out_sum(c - 1, 1)
                if c and c + 1 < NCH:
                    for th in range(2):
                        x1_rest(c + 1, th)
                if c + 2 < NCH:
                    for t in range(T):
                        prefix(c + 2, t)
                    for th in range(2):
                        first_layer(c + 2, th)
                out_sum(c, 0)
            out_sum(NCH - 1, 1)

        @block.tensor
        def _(pe):
            def transpose_w(g):
                pe.wait_ge(w_landed[g], 16)
                for dk in range(HALVES):
                    for a in range(HALVES):
                        last = nc.tensor.transpose(ps[:, g, dk * D + a * P:dk * D + (a + 1) * P],
                                                   w_rows[:, g, a, dk * P:(dk + 1) * P], ident[:, :])
                last.then_inc(wt_in_psum, 1)

            def transpose_x(n):
                pe.wait_ge(x_landed[n % 2], 32 * (n // 2 + 1))
                if n:
                    pe.wait_ge(x_lo_ready, n)
                for k in range(T // 2):
                    for dk in range(HALVES):
                        to = ps[:, XT + dk].rearrange("p (j k b) -> p k j b", j=2, k=T // 2)[:, k]
                        last = nc.tensor.transpose(to, x_rows[:, n % 2, k * D + dk * P:k * D + (dk + 1) * P],
                                                   ident[:, :])
                last.then_inc(xt_in_psum, 1)

            def split_products(to, w_hi, w_lo, c, dk, a, at, start=False, stop=False):
                rows = slice(a * P, (a + 1) * P)
                for n, (w, v) in enumerate(((w_lo, x_hi), (w_hi, x_lo), (w_hi, x_hi))):
                    last = nc.tensor.matmul(to, w[:, dk, rows], at(v[:, c, dk]), start=start and n == 0,
                                            stop=stop and n == 2, skip_group_check=True)
                return last

            def all_cols(v):
                return v

            def gates(n):
                pe.wait_ge(x_hi_ready, n + 1)
                pe.wait_ge(x_lo_ready, n + 1)
                for g in range(2):
                    if n == 0:
                        pe.wait_ge(wt_lo_ready, g + 1)
                    for a in range(HALVES):
                        if n:
                            pe.wait_ge(gate_ready, 4 * (n - 1) + 2 * g + a + 1)
                        for dk in range(HALVES):
                            last = split_products(ps[:, 2 * g + a], wt_hi[:, g], wt_lo[:, g], chunk_of(n), dk, a,
                                                  all_cols, dk == 0, dk == 1)
                        last.then_inc(gate_in_psum, 1)

            def candidate(m):
                if m > EARLY:
                    pe.wait_ge(gate_ready, 4 * NCH)
                before = max((k for k in range(m) if CAND_BANK[k] == CAND_BANK[m]), default=None)
                for a in range(HALVES):
                    if before is not None:
                        if CAND_ORDER[before] in MOVED:
                            pe.wait_ge(cand_moved, 2 * MOVED_ORDER.index(CAND_ORDER[before]) + a + 1)
                        else:
                            pe.wait_ge(w_ready[a], before + 1)
                    for dk in range(HALVES):
                        last = split_products(ps[:, CAND_BANK[m] + a], wt_hi[:, 2], wt_lo[:, 2], CAND_ORDER[m], dk, a,
                                              all_cols, dk == 0, dk == 1)
                    last.then_inc(cand_in_psum, 1)

            pe.wait_ge(ident_ready, 1)
            transpose_w(0)
            transpose_x(0)
            transpose_w(1)
            transpose_w(2)
            pe.wait_ge(cond_landed, 16)
            for a in range(HALVES):
                last = nc.tensor.transpose(ps[:, 3, cols(a)], cond_rows[:, a * P:(a + 1) * P], ident[0:B, 0:B])
            last.then_inc(wt_in_psum, 1)
            pe.wait_ge(wt_lo_ready, 3)
            pe.wait_ge(h0_ready, 2)
            for n in range(NCH):
                if n + 1 < NCH:
                    transpose_x(n + 1)
                gates(n)
                if n in EARLY_AFTER:
                    candidate(EARLY_AFTER[n])
            for m in range(EARLY, NCH):
                candidate(m)

            def project(c, bank, part, steps=slice(0, T // 2), first=True):
                a, par = bank // 2, bank % 2
                n = (steps.stop - steps.start) * B
                to = ps[:, 4 * (c % 2) + bank, steps.start * B:steps.stop * B]
                if part == 0:
                    nc.tensor.matmul(to, bx_part[:, a * P:(a + 1) * P], ones[:, 0:n], start=first, stop=False,
                                     skip_group_check=True)

                def at(v):
                    return v.rearrange("p (s r b) -> p r s b", r=2, b=B)[:, par, steps]

                split_products(to, wx_hi, wx_lo, c, part, a, at)

            def step_part(c, t, dk, a):
                if c or t:
                    before = h_t[:, (c - (t == 0)) % 2, dk, cols((t - 1) % T)]
                else:
                    before = r_d[:, 0, dk, cols(T - 1)]
                return nc.tensor.matmul(ps[:, 4 * (c % 2) + 2 * a + t % 2, cols(t // 2)],
                                        wh_f[:, dk, a * P:(a + 1) * P], before, start=False, stop=dk == 1,
                                        skip_group_check=True)

            def transpose_out(c, k):
                if k == 0:
                    pe.wait_ge(o_ready, 2 * c + 2)
                for a in range(HALVES):
                    last = nc.tensor.transpose(ps[:, 4 * (c % 2) + k, D + a * P:D + (a + 1) * P],
                                               suf[:, c % 2, a, k * P:(k + 1) * P], ident[:, :])
                last.then_inc(o_in_psum, 1)

            def between(c, slot):
                start = 7 if c == 1 else 3
                if c and start <= slot < start + 4:
                    transpose_out(c - 1, slot - start)
                if c + 1 == NCH:
                    return
                if c == 0 and slot in (3, 5, 7, 9):
                    pe.wait_ge(x1_lo_ready, 2)
                    for part in range(2):
                        project(0, (slot - 3) // 2, part, slice(T // 4, T // 2), False)
                if c == 0:
                    parts = {13: (0, 1), 14: (2, 3, 4), 15: (5, 6, 7)}.get(slot, ())
                elif c == 1:
                    parts = {11: (0, 1), 12: (2,), 13: (3, 4), 14: (5,), 15: (6, 7)}.get(slot, ())
                else:
                    parts = (slot - 7,) if 7 <= slot < 15 else ()
                for p in parts:
                    if p == 0:
                        pe.wait_ge(x1_lo_ready, 2 * (c + 1) + 2)
                    if p == 0 and c == 0:
                        pe.wait_ge(w_first_ready, 4)
                        pe.wait_ge(w_second_ready, 2)
                    if c and p in (0, 4):
                        pe.wait_ge(o_rows_ready, 2 * (c - 1) + 1 + p // 4)
                    project(c + 1, p // 2, p % 2)

            pe.wait_ge(cand_moved, 4)
            for done, count in ((suf_steps, T * NCH - 4), (suf_steps, T * NCH), (w_first_ready, 2), (s_steps, 3),
                                (x1_ready, 1)):
                pe.wait_ge(done, count)
                for _ in range(4):
                    nc.tensor.matmul(ps[:, 2], wt_hi[:, 0, 0, 0:P], x_hi[:, NCH - 1, 0], start=True, stop=True,
                                     skip_group_check=True)
            pe.wait_ge(cand_moved, 2 * len(MOVED))
            pe.wait_ge(wt_lo_ready, 4)
            pe.wait_ge(bx_ready, 1)
            pe.wait_ge(wh_landed, 16)
            pe.wait_ge(x1_lo_ready, 1)
            for bank in range(4):
                for part in range(2):
                    project(0, bank, part, slice(0, T // 4), True)
            for c in range(NCH):
                for t in range(T):
                    if c or t:
                        pe.wait_ge(h_ready, HALVES * (T * c + t) - 1)
                    step_part(c, t, 0, 0)
                    between(c, 2 * t)
                    if c or t:
                        pe.wait_ge(h_ready, HALVES * (T * c + t))
                    step_part(c, t, 1, 0).then_inc(z_in_psum, 1)
                    step_part(c, t, 0, 1)
                    step_part(c, t, 1, 1).then_inc(z_in_psum, 1)
                    between(c, 2 * t + 1)
            for k in range(T // 2):
                transpose_out(NCH - 1, k)


_INS = ['x', 'cond_1024', 'L0_cond_W_f', 'L0_cond_b_f', 'L0_cond_W_i', 'L0_cond_b_i', 'L0_cond_W_h', 'L0_cond_b_h',
        'L1_cond_Wx', 'L1_cond_Wh', 'L1_cond_b']


def kernel(**inputs):
    import numpy as np
    import concourse.bacc as bacc
    from concourse.bass_utils import run_bass_kernel_spmd

    nc = bacc.Bacc("TRN2", target_bir_lowering=False, num_devices=1)
    arrays, args = {}, []
    for name in _INS:
        a = np.ascontiguousarray(inputs[name])
        arrays[f"in_{name}"] = a
        args.append(nc.dram_tensor(f"in_{name}", a.shape, mybir.dt.from_np(a.dtype), kind="ExternalInput").ap())
    out = nc.dram_tensor("out_x", (B, S, D), F32, kind="ExternalOutput").ap()
    build(nc, *args, out)
    result = run_bass_kernel_spmd(nc, [arrays], core_ids=[0])
    return result.results[0]["out_x"]
```

```python
from contextlib import ExitStack

import concourse.bass as bass
from concourse import mybir

F32 = mybir.dt.float32
F32R = mybir.dt.float32r
BF16 = mybir.dt.bfloat16
ALU = mybir.AluOpType
ACT = mybir.ActivationFunctionType

P = 128
B = 64
S = 64
D = 256
HALVES = D // P
T = 8
NCH = S // T
COLS = T * B
CH = HALVES * COLS
RING = 4
SUF = 3
EPS = 1e-8
WARM_UP = 9


def build(nc, x, cond, w_f, b_f, w_i, b_i, w_h, b_h, wx, wh, b_x, out):
    with ExitStack() as ctx:
        def sb(name, shape, dt=F32):
            return ctx.enter_context(nc.sbuf_tensor(name, shape, dt))

        def sem(name):
            return ctx.enter_context(nc.semaphore(name))

        x_rows = sb("x_rows", [P, 2, T // 2 * D])
        o_rows = x_rows
        d_first = x_rows[:, 0, :].rearrange("p (a c) -> p a c", a=2)
        x_hi = sb("x_hi", [P, NCH, HALVES, COLS], F32R)
        x_lo = sb("x_lo", [P, NCH, HALVES, COLS], F32R)
        r_d = sb("r_d", [P, NCH + 1, HALVES, COLS])
        q_s = sb("q_s", [P, NCH, HALVES, COLS])
        den = sb("den", [P, RING, HALVES, COLS])
        suf = sb("suf", [P, SUF, HALVES, COLS])
        h_t = sb("h_t", [P, 2, HALVES, COLS])
        w_rows = h_t[:, :, :, :].rearrange("p n a c -> p (n a c)")[:, 0:3 * HALVES * D]\
            .rearrange("p (g a d) -> p g a d", g=3, a=HALVES)
        wt_hi = sb("wt_hi", [P, 3, HALVES, D], F32R)
        wt_lo = sb("wt_lo", [P, 3, HALVES, D], F32R)
        wx_f = sb("wx_f", [P, HALVES, D])
        wx_hi = sb("wx_hi", [P, HALVES, D], F32R)
        wx_lo = sb("wx_lo", [P, HALVES, D], F32R)
        wh_f = sb("wh_f", [P, HALVES, D])
        cond_rows = sb("cond_rows", [B, D])
        bias = sb("bias", [P, 3, HALVES])
        bx_rows = sb("bx_rows", [3, D])
        bx_rest = sb("bx_rest", [3, D])
        bx_part = sb("bx_part", [3, D], BF16)
        bx_part2 = sb("bx_part2", [3, D], BF16)
        bx_3 = sb("bx_3", [3, D], BF16)
        ones = sb("ones", [3, COLS], BF16)
        ident = sb("ident", [P, P])
        eps_col = sb("eps_col", [P, 1])
        first = sb("first", [P, 1])

        ps = ctx.enter_context(nc.psum_tensor("ps", [P, 8, COLS], F32))
        XT, CAND = 4, 6
        WT, H0T, WARM = (0, 6, 7), 3, 2

        x_landed = [sem(f"x_landed{q}") for q in range(2)]
        w_landed = [sem(f"w_landed{g}") for g in range(3)]
        cond_landed = sem("cond_landed")
        wx_landed = sem("wx_landed")
        wh_landed = sem("wh_landed")
        bias_landed = sem("bias_landed")
        bx_landed = sem("bx_landed")
        zeroed = sem("zeroed")
        ident_ready = sem("ident_ready")
        wt_in_psum = sem("wt_in_psum")
        wt_hi_ready = sem("wt_hi_ready")
        wt_lo_ready = sem("wt_lo_ready")
        h0_ready = sem("h0_ready")
        bx_step = sem("bx_step")
        bx_ready = sem("bx_ready")
        xt_in_psum = sem("xt_in_psum")
        x_hi_ready = sem("x_hi_ready")
        x_lo_ready = sem("x_lo_ready")
        gate_in_psum = sem("gate_in_psum")
        gate_ready = sem("gate_ready")
        den_ready = sem("den_ready")
        ln_ready = sem("ln_ready")
        inv_ready = sem("inv_ready")
        u_ready = sem("u_ready")
        r_ready = sem("r_ready")
        r_last_ready = sem("r_last_ready")
        ones_ready = sem("ones_ready")
        suf_steps = sem("suf_steps")
        i_inv_ready = sem("i_inv_ready")
        q_ready = sem("q_ready")
        q_last_ready = sem("q_last_ready")
        cand_in_psum = sem("cand_in_psum")
        w_ready = [sem(f"w_ready{a}") for a in range(HALVES)]
        w_first_ready = sem("w_first_ready")
        w_second_ready = sem("w_second_ready")
        cand_moved = sem("cand_moved")
        w_moved_ready = sem("w_moved_ready")
        s_steps = sem("s_steps")
        d_steps = sem("d_steps")
        x_sum_ready = sem("x_sum_ready")
        xd_ready = sem("xd_ready")
        x1_ready = sem("x1_ready")
        x1_hi_ready = sem("x1_hi_ready")
        x1_lo_ready = sem("x1_lo_ready")
        z_in_psum = sem("z_in_psum")
        h_ready = sem("h_ready")
        o_ready = sem("o_ready")
        o_in_psum = sem("o_in_psum")
        o_rows_ready = sem("o_rows_ready")
        o_last_ready = sem("o_last_ready")
        o_last_in_psum = sem("o_last_in_psum")
        o_last_rows_ready = sem("o_last_rows_ready")
        o_stored = [sem(f"o_stored{q}") for q in range(2)]

        def chunk_rows(tensor, c):
            return tensor[:, c * T:(c + 1) * T, :].rearrange("b (j k) d -> j b (k d)", j=2)

        def cols(t, n=1):
            return slice(t * B, (t + n) * B)

        def half_cols(th):
            return cols(th * T // 2, T // 2)

        def d_of(c):
            return d_first if c == 0 else r_d[:, c + 1]

        def last_out_psum(k):
            at = k % 2 * D if k < 2 else 0
            return ps[:, 4 * (NCH % 2) + (2, 2, 3, 0)[k], at:at + D]

        def chunk_of(n):
            return NCH - 1 - n

        CAND_ORDER = [7, 6, 5, 0, 4, 3, 1, 2]
        CAND_BANK = [CAND, CAND, CAND, XT, 0, 2, CAND, 0]
        EARLY_AFTER = {2: 0, 4: 1, 6: 2}
        EARLY = len(EARLY_AFTER)
        def split_after(c):
            if c == 0:
                return {4: (1, 0), 5: (1, 1)}
            if c == 1:
                return {3: (2, 0), 4: (2, 1)}
            if c == 2:
                return {0: (3, 0), 1: (3, 1), 6: (4, 0), 7: (4, 1)}
            return {5: (c + 2, 0), 6: (c + 2, 1)} if c + 2 < NCH else {}

        OUT_STEPS = [(), (4, 5), (2, 3), (4, 5)]

        TRANSPOSES = [[0] * 16,
                      [0] * 7 + [2] * 4 + [0] * 5,
                      [0] * 3 + [2] * 4 + [0] * 9,
                      [0] * 7 + [2] * 4 + [0] * 5]
        PIECES = [[0] * 13 + [6, 9, 9],
                  [0] * 11 + [6, 3, 6, 3, 6],
                  [0] * 7 + [3] * 6 + [2] * 3,
                  [0] + [2] * 6 + [0] * 4 + [3, 2, 3, 2, 2]]

        MOVED = {4: x_rows[:, 1, :].rearrange("p (a c) -> p a c", a=2), 3: h_t[:, 1], 2: den[:, RING - 1]}
        MOVED_ORDER = list(MOVED)

        block = ctx.enter_context(nc.Block())

        @block.sync
        def _(sp):
            def load_x(n):
                for j in range(2):
                    sp.dma_start(x_rows[j * B:(j + 1) * B, n % 2, :], chunk_rows(x, chunk_of(n))[j])\
                        .then_inc(x_landed[n % 2], 16)

            load_x(0)
            for g, w in enumerate((w_f, w_i)):
                sp.dma_start(w_rows[:, g, :, :], w.rearrange("(a p) d -> p a d", p=P)).then_inc(w_landed[g], 16)
            load_x(1)
            sp.dma_start(w_rows[:, 2, :, :], w_h.rearrange("(a p) d -> p a d", p=P)).then_inc(w_landed[2], 16)
            sp.dma_start(cond_rows[:, :], cond).then_inc(cond_landed, 16)
            sp.dma_start(wx_f[:, :, :], wx.rearrange("(a p) d -> p a d", p=P)).then_inc(wx_landed, 16)
            sp.dma_start(wh_f[:, :, :], wh.rearrange("(a p) d -> p a d", p=P)).then_inc(wh_landed, 16)
            for n in range(2, NCH):
                sp.wait_ge(xt_in_psum, n - 1)
                load_x(n)
            for c in range(NCH - 1):
                sp.wait_ge(o_rows_ready, 2 * c + 2)
                for j in range(2):
                    sp.dma_start(chunk_rows(out, c)[j], o_rows[j * B:(j + 1) * B, c % 2, :])\
                        .then_inc(o_stored[c % 2], 16)
            sp.wait_ge(o_rows_ready, 2 * NCH - 1)
            for k, part in ((1, slice(0, 3 * D)), (2, slice(3 * D, 4 * D))):
                sp.wait_ge(o_last_rows_ready, k)
                for j in range(2):
                    sp.dma_start(chunk_rows(out, NCH - 1)[j][:, part],
                                 o_rows[j * B:(j + 1) * B, (NCH - 1) % 2, part]).then_inc(o_stored[1], 16)
            sp.wait_ge(o_stored[0], 32 * (NCH // 2))
            sp.wait_ge(o_stored[1], 32 * (NCH // 2 + 1))

        @block.gpsimd
        def _(pool):
            nc.gpsimd.memset(ident[:, :], 0.0).then_inc(zeroed, 1)
            pool.wait_ge(zeroed, 1)
            nc.gpsimd.affine_select(out=ident[:, :], in_=ident[:, :], compare_op=ALU.not_equal, fill=1.0,
                                    base=0, pattern=[[-1, P]], channel_multiplier=1).then_inc(ident_ready, 1)

            def i_by_den(n):
                pool.wait_ge(inv_ready, n + 1)
                nc.gpsimd.tensor_tensor(q_s[:, chunk_of(n)], q_s[:, chunk_of(n)], den[:, n % RING], ALU.mult)\
                    .then_inc(i_inv_ready, 1)

            def q_chunk(n):
                pool.wait_ge(i_inv_ready, n + 1)
                pool.wait_ge(suf_steps, T * (n + 1))
                nc.gpsimd.tensor_tensor(q_s[:, chunk_of(n)], q_s[:, chunk_of(n)], suf[:, n % SUF], ALU.mult)\
                    .then_inc(q_ready, 1)

            def x_sum(c):
                pool.wait_ge(x_lo_ready, NCH)
                if c >= RING:
                    pool.wait_ge(o_ready, 2 * (c - RING) + 2)
                else:
                    pool.wait_ge(i_inv_ready, NCH - RING + c + 1 if c < RING // 2 else NCH)
                    pool.wait_ge(u_ready, NCH - RING + c + 1)
                if c == RING - 1:
                    pool.wait_ge(w_moved_ready, MOVED_ORDER.index(2) + 1)
                nc.gpsimd.tensor_tensor(den[:, c % RING], x_hi[:, c].bitcast(F32), x_lo[:, c].bitcast(F32),
                                        ALU.add).then_inc(x_sum_ready, 1)

            def d_half(c, th):
                for t in range(th * T // 2, (th + 1) * T // 2):
                    if c or t:
                        pool.wait_ge(d_steps, T * c + t)
                    before = d_of(c)[:, :, cols(t - 1)] if t else d_of(c - 1)[:, :, cols(T - 1)]
                    nc.gpsimd.tensor_tensor(d_of(c)[:, :, cols(t)], d_of(c)[:, :, cols(t)], before, ALU.mult)\
                        .then_inc(d_steps, 1)
                pool.wait_ge(x_sum_ready, c + 1)
                pool.wait_ge(d_steps, T * c + (th + 1) * T // 2)
                nc.gpsimd.tensor_tensor(den[:, c % RING, :, half_cols(th)], den[:, c % RING, :, half_cols(th)],
                                        d_of(c)[:, :, half_cols(th)], ALU.add).then_inc(xd_ready, 1)

            def plus_eps(n):
                c = chunk_of(n)
                pool.wait_ge(suf_steps, T * (n + 1))
                nc.gpsimd.tensor_scalar(r_d[:, c + 1], r_d[:, c + 1], 1.0, EPS, ALU.mult, ALU.add).then_inc(r_ready, 1)

            i_by_den(0)
            for n in range(NCH - 3):
                i_by_den(n + 1)
                q_chunk(n)
                plus_eps(n)
            x_sum(0)
            x_sum(1)
            i_by_den(NCH - 1)
            pool.wait_ge(r_last_ready, 1)
            pool.wait_ge(h0_ready, 2)
            d_half(0, 0)
            i_by_den(NCH - 2)
            d_half(0, 1)
            pool.wait_ge(r_last_ready, 3)
            d_half(1, 0)
            d_half(1, 1)
            q_chunk(NCH - 3)
            pool.wait_ge(r_ready, NCH - 3)
            for c in range(2, NCH):
                x_sum(c)
                d_half(c, 0)
                d_half(c, 1)

        @block.scalar
        def _(act):
            act.wait_ge(ones_ready, 1)
            nc.scalar.activation(first[:, :], first[:, :], ACT.Sigmoid)
            with nc.allow_non_contiguous_dma(reason="three bias vectors of 1 KB"):
                for g, b in enumerate((b_f, b_i, b_h)):
                    act.dma_start(bias[:, g, :], b.rearrange("(a p) -> p a", p=P)).then_inc(bias_landed, 16)
            for j in range(3):
                act.dma_start(bx_rows[j:j + 1, :], b_x.rearrange("(a n) -> a n", a=1)).then_inc(bx_landed, 16)

            def split_x(n):
                act.wait_ge(xt_in_psum, n + 1)
                nc.scalar.activation(x_hi[:, chunk_of(n)], ps[:, XT:XT + 2], ACT.Copy).then_inc(x_hi_ready, 1)

            def split_w(g):
                act.wait_ge(wt_in_psum, g + 1)
                nc.scalar.activation(wt_hi[:, g], ps[:, WT[g]].rearrange("p (a h) -> p a h", a=HALVES), ACT.Copy)\
                    .then_inc(wt_hi_ready, 1)

            def sigmoids(n):
                c = chunk_of(n)
                for g in range(2):
                    for a in range(HALVES):
                        act.wait_ge(gate_in_psum, 4 * n + 2 * g + a + 1)
                        to = (r_d[:, c + 1, a], q_s[:, c, a])[g]
                        nc.scalar.activation(to, ps[:, 2 * g + a], ACT.Sigmoid, bias=bias[:, g, a:a + 1])\
                            .then_inc(gate_ready, 1)

            def inverses(n):
                nc.scalar.preload_act_table_set("natural_log_exp_and_others")
                for k in range(n, n + 2):
                    act.wait_ge(den_ready, k + 1)
                    nc.scalar.activation(den[:, k % RING], den[:, k % RING], ACT.Ln).then_inc(ln_ready, 1)
                    if k == n and n + 3 < NCH:
                        split_x(n + 3)
                for k in range(n, n + 2):
                    act.wait_ge(ln_ready, k + 1)
                    nc.scalar.activation(den[:, k % RING], den[:, k % RING], ACT.Exp, scale=-1.0)\
                        .then_inc(inv_ready, 1)

            split_w(0)
            split_x(0)
            split_w(1)
            split_w(2)
            act.wait_ge(wt_in_psum, 4)
            for a in range(HALVES):
                nc.scalar.activation(r_d[:, 0, a, cols(T - 1)], ps[:, H0T, cols(a)], ACT.Copy).then_inc(h0_ready, 1)
            act.wait_ge(wx_landed, 16)
            nc.scalar.activation(wx_hi[:, :, :], wx_f[:, :, :], ACT.Copy).then_inc(wt_hi_ready, 1)
            act.wait_ge(bias_landed, 48)
            split_x(1)
            for n in range(0, NCH, 2):
                sigmoids(n)
                if n + 2 < NCH:
                    split_x(n + 2)
                sigmoids(n + 1)
                inverses(n)

            def tanh(c, t):
                if c >= 2 and t == 0:
                    act.wait_ge(o_ready, 2 * (c - 1))
                if c == 1 and t == 0:
                    act.wait_ge(w_moved_ready, MOVED_ORDER.index(3) + 1)
                for a in range(HALVES):
                    act.wait_ge(z_in_psum, HALVES * (T * c + t) + a + 1)
                    nc.scalar.activation(h_t[:, c % 2, a, cols(t)],
                                         ps[:, 4 * (c % 2) + 2 * a + t % 2, cols(t // 2)], ACT.Tanh)\
                        .then_inc(h_ready, 1)

            def split_x1(c, th):
                act.wait_ge(x1_ready, 2 * c + th + 1)
                nc.scalar.activation(x_hi[:, c, :, half_cols(th)], den[:, c % RING, :, half_cols(th)], ACT.Copy)\
                    .then_inc(x1_hi_ready, 1)

            def out_rows(c, part):
                act.wait_ge(o_in_psum, T // 2 * c + 2 * part + 2)
                if c == 1 and part == 0:
                    act.wait_ge(w_moved_ready, MOVED_ORDER.index(4) + 1)
                if c >= 2 and part == 0:
                    act.wait_ge(o_stored[c % 2], 32 * (c // 2))
                nc.scalar.activation(o_rows[:, c % 2, 2 * part * D:2 * (part + 1) * D],
                                     ps[:, 4 * (c % 2) + part], ACT.Copy).then_inc(o_rows_ready, 1)

            def move_candidate(c):
                for a in range(HALVES):
                    m = CAND_ORDER.index(c)
                    act.wait_ge(cand_in_psum, 2 * m + a + 1)
                    nc.scalar.activation(MOVED[c][:, a], ps[:, CAND_BANK[m] + a], ACT.Identity,
                                         bias=bias[:, 2, a:a + 1]).then_inc(cand_moved, 1)

            nc.scalar.preload_act_table_set("sigmoid_and_others")
            act.wait_ge(xt_in_psum, NCH)
            def plus_eps(c):
                if c:
                    act.wait_ge(suf_steps, T * (NCH - c))
                else:
                    act.wait_ge(u_ready, NCH)
                nc.scalar.activation(d_of(c), r_d[:, c + 1], ACT.Identity, bias=eps_col[:, 0:1])\
                    .then_inc(r_last_ready, 1)

            move_candidate(4)
            move_candidate(3)
            plus_eps(0)
            plus_eps(2)
            plus_eps(1)
            act.wait_ge(i_inv_ready, NCH - 1)
            act.wait_ge(u_ready, NCH)
            move_candidate(2)
            split_x1(0, 0)
            split_x1(0, 1)
            for c in range(NCH):
                for t in range(T):
                    tanh(c, t)
                    if t in split_after(c):
                        split_x1(*split_after(c)[t])
                    if t in OUT_STEPS[min(c, 3)]:
                        out_rows(c - 1, OUT_STEPS[min(c, 3)].index(t))
            act.wait_ge(o_last_in_psum, 2)
            act.wait_ge(o_stored[(NCH - 1) % 2], 32 * ((NCH - 1) // 2))
            nc.scalar.activation(o_rows[:, (NCH - 1) % 2, 0:2 * D].rearrange("p (k d) -> p k d", k=2),
                                 ps[:, 4 * (NCH % 2) + 2].rearrange("p (k d) -> p k d", k=2), ACT.Copy)\
                .then_inc(o_rows_ready, 1)

        @block.vector
        def _(dve):
            def chunk_split(n):
                dve.wait_ge(x_hi_ready, n + 1)
                c = chunk_of(n)
                nc.vector.tensor_tensor(x_lo[:, c], ps[:, XT:XT + 2], x_hi[:, c].bitcast(F32), ALU.subtract)\
                    .then_inc(x_lo_ready, 1)

            def weight_split(g):
                dve.wait_ge(wt_hi_ready, g + 1)
                nc.vector.tensor_tensor(wt_lo[:, g], ps[:, WT[g]].rearrange("p (a h) -> p a h", a=HALVES),
                                        wt_hi[:, g].bitcast(F32), ALU.subtract).then_inc(wt_lo_ready, 1)

            def denominator(n):
                c = chunk_of(n)
                dve.wait_ge(gate_ready, 4 * n + 4)
                if n >= RING:
                    dve.wait_ge(i_inv_ready, n - RING + 1)
                nc.vector.scalar_tensor_tensor(den[:, n % RING], r_d[:, c + 1], EPS, q_s[:, c], ALU.add, ALU.add)\
                    .then_inc(den_ready, 1)

            def ratio(n):
                c = chunk_of(n)
                dve.wait_ge(inv_ready, n + 1)
                nc.vector.tensor_tensor(r_d[:, c + 1], r_d[:, c + 1], den[:, n % RING], ALU.mult).then_inc(u_ready, 1)
                dve.wait_ge(u_ready, n + 1)

            def suffix(n, t):
                c = chunk_of(n)
                k = T - 1 - t
                if n >= SUF and k == 0:
                    dve.wait_ge(q_ready, n - SUF + 1)
                if n or k:
                    dve.wait_ge(suf_steps, T * n + k)
                after = suf[:, n % SUF, :, cols(t + 1)] if t < T - 1 else suf[:, (n - 1) % SUF, :, cols(0)]
                nc.vector.scalar_tensor_tensor(suf[:, n % SUF, :, cols(t)], r_d[:, c + 1, :, cols(t)], EPS, after,
                                               ALU.add, ALU.mult).then_inc(suf_steps, 1)

            def weighted(m, a):
                dve.wait_ge(cand_in_psum, 2 * m + a + 1)
                c = CAND_ORDER[m]
                if c >= 2:
                    dve.wait_ge(q_ready, NCH - c)
                else:
                    dve.wait_ge(q_last_ready, 3)
                ready = w_ready[a] if c >= 2 else w_second_ready
                nc.vector.scalar_tensor_tensor(q_s[:, c, a], ps[:, CAND_BANK[m] + a], bias[:, 2, a:a + 1], q_s[:, c, a],
                                               ALU.add, ALU.mult).then_inc(ready, 1)

            def weighted_first(th):
                dve.wait_ge(q_last_ready, 1 + th)
                for a in range(HALVES):
                    dve.wait_ge(cand_in_psum, 2 * CAND_ORDER.index(0) + a + 1)
                    nc.vector.scalar_tensor_tensor(q_s[:, 0, a, half_cols(th)],
                                                   ps[:, CAND_BANK[CAND_ORDER.index(0)] + a, half_cols(th)],
                                                   bias[:, 2, a:a + 1], q_s[:, 0, a, half_cols(th)],
                                                   ALU.add, ALU.mult).then_inc(w_first_ready, 1)

            def q_last(c, th=None):
                at = half_cols(th) if th is not None else slice(0, COLS)
                dve.wait_ge(i_inv_ready, NCH - 1 + c)
                dve.wait_ge(suf_steps, T * NCH)
                nc.vector.tensor_tensor(q_s[:, c, :, at], q_s[:, c, :, at], suf[:, chunk_of(c) % SUF, :, at], ALU.mult)\
                    .then_inc(q_last_ready, 1)

            def prefix(c, t):
                if c == 0 and t == 0:
                    return
                if c or t > 1:
                    dve.wait_ge(s_steps, T * c + t - 1)
                before = q_s[:, c, :, cols(t - 1)] if t else q_s[:, c - 1, :, cols(T - 1)]
                now = q_s[:, c, :, cols(t)]
                nc.vector.tensor_tensor(now, now, before, ALU.add).then_inc(s_steps, 1)

            def first_layer(c, th):
                dve.wait_ge(s_steps, T * c + (th + 1) * T // 2 - 1)
                dve.wait_ge(xd_ready, 2 * c + th + 1)
                nc.vector.tensor_tensor(den[:, c % RING, :, half_cols(th)], den[:, c % RING, :, half_cols(th)],
                                        q_s[:, c, :, half_cols(th)], ALU.add).then_inc(x1_ready, 1)

            def x1_rest(c, th):
                dve.wait_ge(x1_hi_ready, 2 * c + th + 1)
                nc.vector.tensor_tensor(x_lo[:, c, :, half_cols(th)], den[:, c % RING, :, half_cols(th)],
                                        x_hi[:, c, :, half_cols(th)].bitcast(F32), ALU.subtract)\
                    .then_inc(x1_lo_ready, 1)

            def out_sum(c, th):
                dve.wait_ge(h_ready, HALVES * (T * c + (th + 1) * T // 2))
                if c >= 2 and th == 0:
                    dve.wait_ge(o_in_psum, T // 2 * (c - 1))
                to = suf[:, c % 2].rearrange("p a (k j b) -> p j a k b", j=2, k=T // 2)[:, th]
                x1 = den[:, c % RING, :, half_cols(th)].rearrange("p a (k b) -> p a k b", b=B)
                h = h_t[:, c % 2, :, half_cols(th)].rearrange("p a (k b) -> p a k b", b=B)
                nc.vector.tensor_tensor(to, x1, h, ALU.add).then_inc(o_ready, 1)

            def out_sum_last(k):
                c, t = NCH - 1, T // 2 + k
                dve.wait_ge(h_ready, HALVES * (T * c + t + 1))
                nc.vector.tensor_tensor(suf[:, c % 2, :, cols(2 * k + 1)], den[:, c % RING, :, cols(t)],
                                        h_t[:, c % 2, :, cols(t)], ALU.add).then_inc(o_last_ready, 1)

            nc.vector.memset(first[:, :], 0.0).then_inc(ones_ready, 1)
            nc.vector.memset(eps_col[:, :], EPS).then_inc(ones_ready, 1)
            nc.vector.memset(ones[:, :], 1.0).then_inc(ones_ready, 1)
            nc.vector.memset(suf[:, SUF - 1, :, cols(0)], 1.0).then_inc(ones_ready, 1)
            weight_split(0)
            chunk_split(0)
            weight_split(1)
            weight_split(2)

            dve.wait_ge(ones_ready, 4)

            def product(m):
                for a in range(HALVES):
                    weighted(m, a)

            def suffixes(n):
                for t in range(T - 1, -1, -1):
                    suffix(n, t)

            chunk_split(1)
            dve.wait_ge(wt_hi_ready, 4)
            nc.vector.tensor_tensor(wx_lo[:, :, :], wx_f[:, :, :], wx_hi[:, :, :].bitcast(F32), ALU.subtract)\
                .then_inc(wt_lo_ready, 1)

            steps = [0]

            def bx(ins):
                steps[0] += 1
                ins.then_inc(bx_step, 1)
                dve.wait_ge(bx_step, steps[0])

            dve.wait_ge(bx_landed, 48)
            dve.wait_ge(ident_ready, 1)
            bx(nc.vector.tensor_copy(bx_part[:, :], bx_rows[:, :]))
            bx(nc.vector.tensor_scalar(bx_3[:, :], bx_part[:, :], ident[0:3, 0:1], None, ALU.mult))
            rest = bx_rows
            for j in (1, 2):
                bx(nc.vector.tensor_tensor(bx_rest[:, :], rest[:, :], bx_part[:, :], ALU.subtract))
                bx(nc.vector.tensor_copy(bx_part[:, :], bx_rest[:, :]))
                bx(nc.vector.tensor_scalar(bx_part2[:, :], bx_part[:, :], ident[0:3, j:j + 1], None, ALU.mult))
                bx(nc.vector.tensor_tensor(bx_3[:, :], bx_3[:, :], bx_part2[:, :], ALU.add))
                rest = bx_rest
            nc.vector.tensor_copy(bx_part[:, :], bx_3[:, :]).then_inc(bx_ready, 1)

            for n in range(0, NCH, 2):
                if n:
                    ratio(n - 2)
                denominator(n)
                if n + 2 < NCH:
                    chunk_split(n + 2)
                if n:
                    suffixes(n - 2)
                if n >= 4:
                    product(n // 2 - 1)
                denominator(n + 1)
                if n + 3 < NCH:
                    chunk_split(n + 3)
                if n == 2:
                    product(0)
                if n:
                    ratio(n - 1)
                    suffixes(n - 1)
            ratio(NCH - 2)
            ratio(NCH - 1)
            suffixes(NCH - 2)
            suffixes(NCH - 1)
            for th in range(2):
                q_last(0, th)
                weighted_first(th)
                for t in range(th * T // 2, (th + 1) * T // 2):
                    if t == 1 or t == T // 2:
                        dve.wait_ge(w_first_ready, 2 * th + 2)
                    prefix(0, t)
                first_layer(0, th)
                x1_rest(0, th)
            q_last(1)
            product(CAND_ORDER.index(1))
            dve.wait_ge(w_second_ready, 2)
            for t in range(T):
                prefix(1, t)
            for th in range(2):
                first_layer(1, th)
            for th in range(2):
                x1_rest(1, th)
            for n, c in enumerate(MOVED_ORDER):
                dve.wait_ge(cand_moved, 2 * n + 2)
                dve.wait_ge(q_ready, NCH - c)
                nc.vector.tensor_tensor(q_s[:, c], q_s[:, c], MOVED[c], ALU.mult).then_inc(w_moved_ready, 1)
            dve.wait_ge(w_moved_ready, 3)
            for c in range(NCH):
                if c:
                    out_sum(c - 1, 1)
                if c in (1, 2):
                    for th in range(2):
                        x1_rest(c + 1, th)
                if c + 2 < NCH:
                    for t in range(T):
                        prefix(c + 2, t)
                    for th in range(2):
                        first_layer(c + 2, th)
                out_sum(c, 0)
                if c >= 2 and c + 2 < NCH:
                    for th in range(2):
                        x1_rest(c + 2, th)
            for k in range(T // 2):
                out_sum_last(k)
            dve.wait_ge(o_stored[(NCH - 1) % 2], 32 * ((NCH - 1) // 2))
            for k in (2, 3):
                dve.wait_ge(o_last_in_psum, k + 1)
                nc.vector.tensor_copy(o_rows[:, (NCH - 1) % 2, k * D:(k + 1) * D], last_out_psum(k))\
                    .then_inc(o_last_rows_ready, 1)

        @block.tensor
        def _(pe):
            def transpose_w(g):
                pe.wait_ge(w_landed[g], 16)
                for dk in range(HALVES):
                    for a in range(HALVES):
                        last = nc.tensor.transpose(ps[:, WT[g], dk * D + a * P:dk * D + (a + 1) * P],
                                                   w_rows[:, g, a, dk * P:(dk + 1) * P], ident[:, :])
                last.then_inc(wt_in_psum, 1)

            def transpose_x(n):
                pe.wait_ge(x_landed[n % 2], 32 * (n // 2 + 1))
                if n:
                    pe.wait_ge(x_lo_ready, n)
                for k in range(T // 2):
                    for dk in range(HALVES):
                        to = ps[:, XT + dk].rearrange("p (j k b) -> p k j b", j=2, k=T // 2)[:, k]
                        last = nc.tensor.transpose(to, x_rows[:, n % 2, k * D + dk * P:k * D + (dk + 1) * P],
                                                   ident[:, :])
                last.then_inc(xt_in_psum, 1)

            def split_products(to, w_hi, w_lo, c, dk, a, at, start=False, stop=False):
                rows = slice(a * P, (a + 1) * P)
                for n, (w, v) in enumerate(((w_lo, x_hi), (w_hi, x_lo), (w_hi, x_hi))):
                    last = nc.tensor.matmul(to, w[:, dk, rows], at(v[:, c, dk]), start=start and n == 0,
                                            stop=stop and n == 2, skip_group_check=True)
                return last

            def all_cols(v):
                return v

            def gates(n):
                pe.wait_ge(x_hi_ready, n + 1)
                pe.wait_ge(x_lo_ready, n + 1)
                for g in range(2):
                    if n == 0:
                        pe.wait_ge(wt_lo_ready, g + 1)
                    if n == 0 and g == 1:
                        pe.wait_ge(h0_ready, 2)
                    for a in range(HALVES):
                        if n:
                            pe.wait_ge(gate_ready, 4 * (n - 1) + 2 * g + a + 1)
                        for dk in range(HALVES):
                            last = split_products(ps[:, 2 * g + a], wt_hi[:, g], wt_lo[:, g], chunk_of(n), dk, a,
                                                  all_cols, dk == 0, dk == 1)
                        last.then_inc(gate_in_psum, 1)

            def candidate(m):
                if m == 0:
                    pe.wait_ge(wt_lo_ready, 3)
                if m > EARLY:
                    pe.wait_ge(gate_ready, 4 * NCH)
                before = max((k for k in range(m) if CAND_BANK[k] == CAND_BANK[m]), default=None)
                for a in range(HALVES):
                    if before is not None:
                        if CAND_ORDER[before] in MOVED:
                            pe.wait_ge(cand_moved, 2 * MOVED_ORDER.index(CAND_ORDER[before]) + a + 1)
                        else:
                            pe.wait_ge(w_ready[a], before + 1)
                    for dk in range(HALVES):
                        last = split_products(ps[:, CAND_BANK[m] + a], wt_hi[:, 2], wt_lo[:, 2], CAND_ORDER[m], dk, a,
                                              all_cols, dk == 0, dk == 1)
                    last.then_inc(cand_in_psum, 1)

            pe.wait_ge(ident_ready, 1)
            for _ in range(WARM_UP):
                nc.tensor.matmul(ps[:, WARM, 0:P], ident[:, :], ident[:, :], start=True, stop=True,
                                 skip_group_check=True)
            transpose_w(0)
            transpose_x(0)
            transpose_w(1)
            transpose_w(2)
            pe.wait_ge(cond_landed, 16)
            for a in range(HALVES):
                last = nc.tensor.transpose(ps[:, H0T, cols(a)], cond_rows[:, a * P:(a + 1) * P], ident[0:B, 0:B])
            last.then_inc(wt_in_psum, 1)
            for n in range(NCH):
                if n + 1 < NCH:
                    transpose_x(n + 1)
                gates(n)
                if n in EARLY_AFTER:
                    candidate(EARLY_AFTER[n])
            for m in range(EARLY, NCH):
                candidate(m)

            def project(c, i, steps=slice(0, T // 2), first=True):
                bank, part, pair = (2, 3, 0, 1)[i // 6], i // 3 % 2, i % 3
                a, par = bank // 2, bank % 2
                to = ps[:, 4 * (c % 2) + bank, steps.start * B:steps.stop * B]
                w, v = ((wx_lo, x_hi), (wx_hi, x_lo), (wx_hi, x_hi))[pair]
                moving = v[:, c, part].rearrange("p (s r b) -> p r s b", r=2, b=B)[:, par, steps]
                if i % 6 == 0:
                    nc.tensor.matmul(to, bx_part[:, a * P:(a + 1) * P], ones[:, 0:(steps.stop - steps.start) * B],
                                     start=first, stop=False, skip_group_check=True)
                nc.tensor.matmul(to, w[:, part, a * P:(a + 1) * P], moving, start=False, stop=False,
                                 skip_group_check=True)

            def step_part(c, t, dk, a):
                if c or t:
                    before = h_t[:, (c - (t == 0)) % 2, dk, cols((t - 1) % T)]
                else:
                    before = r_d[:, 0, dk, cols(T - 1)]
                return nc.tensor.matmul(ps[:, 4 * (c % 2) + 2 * a + t % 2, cols(t // 2)],
                                        wh_f[:, dk, a * P:(a + 1) * P], before, start=False, stop=dk == 1,
                                        skip_group_check=True)

            def transpose_out(c, i):
                k, a = i // HALVES, i % HALVES
                if i == 0:
                    pe.wait_ge(o_ready, 2 * c + 2)
                at = k % 2 * D + a * P
                last = nc.tensor.transpose(ps[:, 4 * (c % 2) + k // 2, at:at + P],
                                           suf[:, c % 2, a, k * P:(k + 1) * P], ident[:, :])
                if a == HALVES - 1:
                    last.then_inc(o_in_psum, 1)

            def keep_warm(bank, count, n):
                for _ in range(count):
                    nc.tensor.matmul(ps[:, bank, 0:n], wt_hi[:, 0, 0, 0:P], x_hi[:, NCH - 1, 0, 0:n],
                                     start=True, stop=True, skip_group_check=True)

            def transpose_last(k):
                if k == 0:
                    pe.wait_ge(o_ready, 2 * (NCH - 1) + 1)
                    pe.wait_ge(o_rows_ready, 2 * (NCH - 1))
                pe.wait_ge(o_last_ready, k + 1)
                for a in range(HALVES):
                    last = nc.tensor.transpose(last_out_psum(k)[:, a * P:(a + 1) * P],
                                               suf[:, (NCH - 1) % 2, a, k * P:(k + 1) * P], ident[:, :])
                last.then_inc(o_last_in_psum, 1)

            def between(c, slot):
                if c == 0 and slot in (3, 5, 7, 9):
                    pe.wait_ge(x1_lo_ready, 2)
                    bank = (slot - 3) // 2
                    for i in range(6):
                        project(0, (2, 3, 0, 1).index(bank) * 6 + i, slice(T // 4, T // 2), False)
                if c and slot % 2 and slot < 14 and not TRANSPOSES[min(c, 3)][slot] and (
                        c == NCH - 1 or not PIECES[min(c, 3)][slot]):
                    keep_warm(4 * ((c + 1) % 2) + 3, 2, P)
                if c == NCH - 1 and slot in (14, 15):
                    transpose_last(slot - 14)
                done = sum(TRANSPOSES[min(c, 3)][:slot])
                for i in range(done, done + TRANSPOSES[min(c, 3)][slot]):
                    transpose_out(c - 1, i)
                done = sum(PIECES[min(c, 3)][:slot])
                for i in range(done, done + PIECES[min(c, 3)][slot] if c + 1 < NCH else done):
                    if i == 0:
                        pe.wait_ge(x1_lo_ready, 2 * (c + 1) + 2)
                        if c == 0:
                            pe.wait_ge(w_first_ready, 4)
                            pe.wait_ge(w_second_ready, 2)
                    if c and i in (12, 18):
                        pe.wait_ge(o_rows_ready, 2 * (c - 1) + i // 6 - 1)
                    project(c + 1, i)

            pe.wait_ge(cand_moved, 4)
            for done, count in ((suf_steps, T * NCH - 4), (suf_steps, T * NCH), (w_first_ready, 2), (s_steps, 3),
                                (x1_ready, 1)):
                pe.wait_ge(done, count)
                keep_warm(2, 4, COLS)
            pe.wait_ge(cand_moved, 2 * len(MOVED))
            pe.wait_ge(wt_lo_ready, 4)
            pe.wait_ge(bx_ready, 1)
            pe.wait_ge(wh_landed, 16)
            pe.wait_ge(x1_lo_ready, 1)
            for i in range(24):
                project(0, i, slice(0, T // 4))
            for c in range(NCH):
                for t in range(T):
                    if c or t:
                        pe.wait_ge(h_ready, HALVES * (T * c + t) - 1)
                    step_part(c, t, 0, 0)
                    step_part(c, t, 0, 1)
                    between(c, 2 * t)
                    if c or t:
                        pe.wait_ge(h_ready, HALVES * (T * c + t))
                    step_part(c, t, 1, 0).then_inc(z_in_psum, 1)
                    step_part(c, t, 1, 1).then_inc(z_in_psum, 1)
                    between(c, 2 * t + 1)
            transpose_last(2)
            transpose_last(3)


_INS = ['x', 'cond_1024', 'L0_cond_W_f', 'L0_cond_b_f', 'L0_cond_W_i', 'L0_cond_b_i', 'L0_cond_W_h', 'L0_cond_b_h',
        'L1_cond_Wx', 'L1_cond_Wh', 'L1_cond_b']


def kernel(**inputs):
    import numpy as np
    import concourse.bacc as bacc
    from concourse.bass_utils import run_bass_kernel_spmd

    nc = bacc.Bacc("TRN2", target_bir_lowering=False, num_devices=1)
    arrays, args = {}, []
    for name in _INS:
        a = np.ascontiguousarray(inputs[name])
        arrays[f"in_{name}"] = a
        args.append(nc.dram_tensor(f"in_{name}", a.shape, mybir.dt.from_np(a.dtype), kind="ExternalInput").ap())
    out = nc.dram_tensor("out_x", (B, S, D), F32, kind="ExternalOutput").ap()
    build(nc, *args, out)
    result = run_bass_kernel_spmd(nc, [arrays], core_ids=[0])
    return result.results[0]["out_x"]
```
